# Optimizing a Trainium2 kernel written in Bass

```python
import numpy as np
import jax
import jax.numpy as jnp

def _softmax(x, axis=-1):
    return jax.nn.softmax(x, axis=axis)

def _gelu(x):
    return jax.nn.gelu(x, approximate=True)

def _silu(x):
    return jax.nn.silu(x)

def _sigmoid(x):
    return jax.nn.sigmoid(x)

def _layernorm(x, axis=-1, eps=1e-05):
    m = jnp.mean(x, axis=axis, keepdims=True)
    v = jnp.var(x, axis=axis, keepdims=True)
    return (x - m) / jnp.sqrt(v + eps)

def _scatter_add(tgt, idx, src, axis=0):
    return tgt.at[idx].add(src)

def _segment_sum(src, seg, n):
    return jax.ops.segment_sum(src, seg, n)
kernel_name = 'mk_cond_resid_d4_seqx_r4_f21a11'

def setup_inputs(seed: int=0):
    np.random.seed(seed)
    _w = jnp.asarray

    def _rec_inputs():
        import jax
        import jax.numpy as jnp
        _rk = jax.random.key(seed)
        x = -0.000125 + 0.9999 * jax.random.normal(jax.random.fold_in(_rk, 1), (128, 64, 512), jnp.float32)
        _lenS = 64 - jax.random.randint(jax.random.fold_in(_rk, 7), (128,), 0, max(1, 64 // 4) + 1, jnp.int32)
        _lenS2 = 64 - jax.random.randint(jax.random.fold_in(_rk, 8), (128,), 0, max(1, 64 // 4) + 1, jnp.int32)
        itok_B_0_7 = jax.random.randint(jax.random.fold_in(_rk, 11), (128,), 0, 8, jnp.int32)
        fside_8xS_0 = -0.00162727 + 0.0609077 * jax.random.normal(jax.random.fold_in(_rk, 12), (8, 64), jnp.float32)
        itok_B_0_3 = jax.random.randint(jax.random.fold_in(_rk, 13), (128,), 0, 4, jnp.int32)
        itok_B_1_198 = jax.random.randint(jax.random.fold_in(_rk, 14), (128,), 1, 199, jnp.int32)
        itok_B_0_6 = jax.random.randint(jax.random.fold_in(_rk, 15), (128,), 0, 7, jnp.int32)
        return (x, itok_B_0_7, fside_8xS_0, itok_B_0_3, itok_B_1_198, itok_B_0_6)
    x, itok_B_0_7, fside_8xS_0, itok_B_0_3, itok_B_1_198, itok_B_0_6 = _rec_inputs()

    def _L0_cond_setup():
        import jax, jax.numpy as jnp
        import numpy as np
        B, C, T = (64, 64, 512)
        D, N = (64, 8)
        key = jax.random.key(seed)
        k_x, k_s, k_w, k_b = jax.random.split(key, 4)
        scale = 1.0 / np.sqrt(C)
        x = jax.random.normal(k_x, (B, C, T), dtype=jnp.float32)
        subjects = jax.random.randint(k_s, (B,), 0, N, dtype=jnp.int64)
        weights = jax.random.normal(k_w, (N, C, D), dtype=jnp.float32) * scale
        bias = jax.random.normal(k_b, (N, D), dtype=jnp.float32) * scale
        return {'x': x, 'subjects': subjects, 'weights': weights, 'bias': bias}
    _L0_cond_all = _L0_cond_setup()
    _L0_cond_in = {k: v for k, v in _L0_cond_all.items() if k in ('weights',)}
    del _L0_cond_all

    def _L1_cond_setup():
        import jax, jax.numpy as jnp
        import numpy as np
        B, S, D_IN, D_OUT, R, E = (8, 512, 512, 512, 16, 4)
        key = jax.random.key(seed)
        ks = jax.random.split(key, 7)
        x = jax.random.normal(ks[0], (B, S, D_IN), dtype=jnp.float32)
        W_base = jax.random.normal(ks[1], (D_OUT, D_IN), dtype=jnp.float32) * 0.02
        Wt = jax.random.normal(ks[2], (D_IN, D_IN), dtype=jnp.float32) * 0.02
        A = jax.random.normal(ks[3], (E, R, D_IN), dtype=jnp.float32) * 0.02
        B_w = jax.random.normal(ks[4], (E, D_OUT, R), dtype=jnp.float32) * 0.02
        Wp = jax.random.normal(ks[5], (D_OUT, D_OUT), dtype=jnp.float32) * 0.02
        scaling = jnp.ones((E,), dtype=jnp.float32)
        adapter_idx = jax.random.randint(ks[6], (B,), 0, E)
        return {'x': x, 'W_base': W_base, 'Wt': Wt, 'A': A, 'B_w': B_w, 'Wp': Wp, 'scaling': scaling, 'adapter_idx': adapter_idx}
    _L1_cond_all = _L1_cond_setup()
    _L1_cond_in = {k: v for k, v in _L1_cond_all.items() if k in ('W_base', 'Wt', 'A', 'B_w', 'Wp', 'scaling')}
    del _L1_cond_all

    def _L2_cond_setup():
        import jax, jax.numpy as jnp
        import numpy as np
        B, C, T = (128, 64, 512)
        S, D = (200, 64)
        key = jax.random.key(seed)
        k1, k2, k3 = jax.random.split(key, 3)
        x = jax.random.normal(k1, (B, C, T), dtype=jnp.float32)
        conditions = jax.random.randint(k2, (B,), 0, S, dtype=jnp.int64)
        weights = jax.random.normal(k3, (S, C, D), dtype=jnp.float32) / jnp.sqrt(jnp.float32(C))
        return {'x': x, 'conditions': conditions, 'weights': weights}
    _L2_cond_all = _L2_cond_setup()
    _L2_cond_in = {k: v for k, v in _L2_cond_all.items() if k in ('weights',)}
    del _L2_cond_all

    def _L3_cond_setup():
        import jax, jax.numpy as jnp
        import numpy as np
        B, T, D_IN, D_OUT = (16, 512, 512, 512)
        N_ADAPTERS, RANK = (8, 16)
        key = jax.random.key(seed)
        k_x, k_w, k_a, k_b, k_s, k_idx = jax.random.split(key, 6)
        x = jax.random.normal(k_x, (B, T, D_IN), dtype=jnp.float32)
        W = jax.random.normal(k_w, (D_OUT, D_IN), dtype=jnp.float32) * (1.0 / np.sqrt(D_IN))
        A = jax.random.normal(k_a, (N_ADAPTERS, RANK, D_IN), dtype=jnp.float32) * 0.02
        Bm = jax.random.normal(k_b, (N_ADAPTERS, D_OUT, RANK), dtype=jnp.float32) * 0.02
        scalings = jnp.ones((N_ADAPTERS,), dtype=jnp.float32)
        adapter_idx = jax.random.randint(k_idx, (B,), 0, N_ADAPTERS, dtype=jnp.int32)
        return {'x': x, 'W': W, 'A': A, 'Bm': Bm, 'scalings': scalings, 'adapter_idx': adapter_idx}
    _L3_cond_all = _L3_cond_setup()
    _L3_cond_in = {k: v for k, v in _L3_cond_all.items() if k in ('W', 'A', 'Bm', 'scalings')}
    del _L3_cond_all
    return {'x': x, 'itok_B_0_7': itok_B_0_7, 'fside_8xS_0': fside_8xS_0, 'itok_B_0_3': itok_B_0_3, 'itok_B_1_198': itok_B_1_198, 'itok_B_0_6': itok_B_0_6, 'L0_cond_weights': _L0_cond_in['weights'], 'L1_cond_W_base': _L1_cond_in['W_base'], 'L1_cond_Wt': _L1_cond_in['Wt'], 'L1_cond_A': _L1_cond_in['A'], 'L1_cond_B_w': _L1_cond_in['B_w'], 'L1_cond_Wp': _L1_cond_in['Wp'], 'L1_cond_scaling': _L1_cond_in['scaling'], 'L2_cond_weights': _L2_cond_in['weights'], 'L3_cond_W': _L3_cond_in['W'], 'L3_cond_A': _L3_cond_in['A'], 'L3_cond_Bm': _L3_cond_in['Bm'], 'L3_cond_scalings': _L3_cond_in['scalings']}

def reference(x, itok_B_0_7, fside_8xS_0, itok_B_0_3, itok_B_1_198, itok_B_0_6, L0_cond_weights, L1_cond_W_base, L1_cond_Wt, L1_cond_A, L1_cond_B_w, L1_cond_Wp, L1_cond_scaling, L2_cond_weights, L3_cond_W, L3_cond_A, L3_cond_Bm, L3_cond_scalings):
    import jax
    import jax.numpy as jnp

    def _L0_cond_ref(x, subjects, weights, bias):
        import jax, jax.numpy as jnp
        import numpy as np
        B, C, T = (64, 64, 512)
        D, N = (64, 8)
        w = weights[subjects]
        b = bias[subjects]
        out = jnp.einsum('bct,bcd->bdt', x, w)
        out = out + b[:, :, None]
        return out

    def _L1_cond_ref(x, W_base, Wt, A, B_w, Wp, scaling, adapter_idx):
        import jax, jax.numpy as jnp
        import numpy as np
        B, S, D_IN, D_OUT, R, E = (8, 512, 512, 512, 16, 4)
        base = jnp.einsum('bsi,oi->bso', x, W_base)
        h = jnp.einsum('bsi,ji->bsj', x, Wt)
        Ab = A[adapter_idx]
        Bb = B_w[adapter_idx]
        sc = scaling[adapter_idx]
        z = jnp.einsum('bsj,brj->bsr', h, Ab)
        l = jnp.einsum('bsr,bor->bso', z, Bb)
        lora_out = jnp.einsum('bso,po->bsp', l, Wp) * sc[:, None, None]
        return base + lora_out

    def _L2_cond_ref(x, conditions, weights):
        import jax, jax.numpy as jnp
        import numpy as np
        B, C, T = (128, 64, 512)
        S, D = (200, 64)
        w = weights[conditions]
        return jnp.einsum('bct,bcd->bdt', x, w)

    def _L3_cond_ref(x, W, A, Bm, scalings, adapter_idx):
        import jax, jax.numpy as jnp
        import numpy as np
        B, T, D_IN, D_OUT = (16, 512, 512, 512)
        N_ADAPTERS, RANK = (8, 16)
        H = jnp.einsum('btd,od->bto', x, W)
        A_b = A[adapter_idx]
        B_b = Bm[adapter_idx]
        s_b = scalings[adapter_idx]
        xa = jnp.einsum('btd,brd->btr', x, A_b)
        delta = jnp.einsum('btr,bor->bto', xa, B_b)
        delta = jax.lax.stop_gradient(delta * s_b[:, None, None])
        return H + delta
    x = x + _L0_cond_ref(x, itok_B_0_7, L0_cond_weights, fside_8xS_0)
    x = x + _L1_cond_ref(x, L1_cond_W_base, L1_cond_Wt, L1_cond_A, L1_cond_B_w, L1_cond_Wp, L1_cond_scaling, itok_B_0_3)
    x = x + _L2_cond_ref(x, itok_B_1_198, L2_cond_weights)
    x = x + _L3_cond_ref(x, L3_cond_W, L3_cond_A, L3_cond_Bm, L3_cond_scalings, itok_B_0_6)
    return x

_drawn_inputs = setup_inputs


def setup_inputs(seed=0):
    import zlib

    import numpy as np

    out = dict(_drawn_inputs(seed))
    spreads = {'L1_cond_scaling': (1.0, 0.6), 'L3_cond_scalings': (1.0, 0.6)}
    factors = {'L1_cond_Wt': 8.0,
     'L1_cond_A': 8.0,
     'L1_cond_B_w': 8.0,
     'L1_cond_Wp': 8.0,
     'L1_cond_W_base': 4.93}
    for name, (base, spread) in spreads.items():
        noise = np.random.default_rng([zlib.crc32(name.encode()), seed]).standard_normal(out[name].shape)
        drawn = base * np.exp(spread * noise) if base else spread * noise
        out[name] = jnp.asarray(drawn.astype(out[name].dtype))
    for name, factor in factors.items():
        out[name] = (out[name] * factor).astype(out[name].dtype)
    return out
```

```python
from contextlib import ExitStack

import concourse.bass as bass
import numpy as np
from concourse import mybir
from concourse.alu_op_type import AluOpType as ALU

B, C, T = 128, 64, 512
NS, NC = 8, 200
E1, E3, RK = 4, 8, 16
COMBOS = E1 * E3
KT = T // 128
RB = 2 * RK
PAIRS = B // 2
GP = 4
GROUPS = PAIRS // GP
PEEL = 2

f32, f32r, i32 = mybir.dt.float32, mybir.dt.float32r, mybir.dt.int32
COPY = mybir.ActivationFunctionType.Copy
EN = mybir.EngineType


def need(engine, semaphore, value):
    if not isinstance(value, int) or value > 0:
        engine.wait_ge(semaphore, value)


def every_group(nc, engine_type, step):
    for h in range(PEEL):
        step(h, h % 2)
    with nc.Fori(PEEL // 2, (GROUPS - PEEL) // 2, engines=(engine_type,)) as two:
        for parity in range(2):
            step(two * 2 + parity, parity)
    for h in range(GROUPS - PEEL, GROUPS):
        step(h, h % 2)


def before_end(h, ahead, end=GROUPS):
    return not isinstance(h, int) or h + ahead < end


def group_use(h, parity):
    return (h + 2 - parity) // 2


def build(nc, x, idx_w, combo_parts, subjects, bias, w0t, w2, wbase, w3t, wt, wpt, a1t, bwt, a3t, bmt,
          scale1, scale3, out):
    r_table = nc.dram_tensor("r_table", [COMBOS, 2, RB, T], f32).ap()
    combo_dram = nc.dram_tensor("combo_dram", [GROUPS, 2 * GP], i32).ap()

    ctx = ExitStack()
    with ctx:
        def sb(name, shape, dt=f32):
            return ctx.enter_context(nc.sbuf_tensor(name, shape, dt))

        def sem(name):
            return ctx.enter_context(nc.semaphore(name))

        bank = [ctx.enter_context(nc.psum_tensor(f"bank{i}", [128, 512], f32)) for i in range(8)]
        yt_ps, z_ps, out_ps, l_ps, beta_ps = bank[0:2], bank[2:4], bank[4:6], bank[6], bank[7]

        wbase_sb = sb("wbase_sb", [128, KT, T])
        n3_sb = sb("n3_sb", [128, KT, T])
        wt_sb = sb("wt_sb", [128, KT, T])
        wpt_sb = sb("wpt_sb", [128, KT, T])
        a1t_sb = sb("a1t_sb", [128, KT, E1 * RK])
        bwt_sb = sb("bwt_sb", [128, KT, E1 * RK])
        a3t_sb = sb("a3t_sb", [128, KT, E3 * RK])
        q3_sb = sb("q3_sb", [128, T])
        scale1_sb = sb("scale1_sb", [128, E1])
        scale3_sb = sb("scale3_sb", [128, 1])
        bias_sb = sb("bias_sb", [NS, 2, C])
        subj_i = sb("subj_i", [NS, B], i32)
        subj_f = sb("subj_f", [NS, B])
        row_i = sb("row_i", [128, 1], i32)
        row_f = sb("row_f", [128, 1])
        onehot = sb("onehot", [NS, B])
        parts_sb = sb("parts_sb", [1, 2, B], i32)
        combo_sb = sb("combo_sb", [1, B], i32)
        ident = sb("ident", [128, 128])
        own_half = sb("own_half", [128, 128])
        own_adapter = sb("own_adapter", [128, E3])
        q_sb = sb("q_sb", [128, KT, 2, E1 * RK])
        qn_sb = sb("qn_sb", [128, T])
        qa_sb = sb("qa_sb", [128, E3, E1 * RK])
        r_f, r_hi, r_lo = wpt_sb[:, :, :], wbase_sb[:, :, :].bitcast(f32r), wt_sb[:, :, :].bitcast(f32r)
        q3_hi = sb("q3_hi", [128, T], f32r)
        q3_lo = sb("q3_lo", [128, T], f32r)
        n13 = sb("n13", [128, KT, 2, T], f32r)
        pg_f = sb("pg_f", [128, KT, (E1 + E3) * RK])
        pg = sb("pg", [128, 2, KT, (E1 + E3) * RK], f32r)
        u_table = sb("u_table", [128, COMBOS, KT, 2, RB], f32r)
        bias_cols = sb("bias_cols", [128, PAIRS])
        widx_sb = sb("widx_sb", [1, 2, 2 * GP], i32)
        ridx_sb = sb("ridx_sb", [1, 2 * GP], i32)
        x_sb = [sb(f"x_sb{i}", [128, GP, T]) for i in range(2)]
        w0_in = [sb(f"w0_in{i}", [128, GP, 128]) for i in range(2)]
        w2_in = [sb(f"w2_in{i}", [128, GP, 128]) for i in range(2)]
        w0_i = [sb(f"w0_i{i}", [128, GP, 128]) for i in range(2)]
        w2_i = [sb(f"w2_i{i}", [128, GP, 128]) for i in range(2)]
        bias_b = [sb(f"bias_b{i}", [128, GP, 128]) for i in range(2)]
        l_sb = [sb(f"l_sb{i}", [128, GP, 128]) for i in range(2)]
        beta_sb = [sb(f"beta_sb{i}", [128, GP, 128]) for i in range(2)]
        r_sb = [sb(f"r_sb{i}", [128, T], f32r) for i in range(2 * GP)]
        y_f = [sb(f"y_f{i}", [128, KT, 128]) for i in range(2)]
        y_sb = [sb(f"y_sb{i}", [128, KT, 2, 128], f32r) for i in range(2)]
        u_sb = [sb(f"u_sb{i}", [128, KT, 2, 2, RB], f32r) for i in range(2)]
        zx = [sb(f"zx{i}", [128, 256]) for i in range(2)]
        zw = [sb(f"zw{i}", [128, 256]) for i in range(2)]
        zs = [sb(f"zs{i}", [128, 128]) for i in range(2)]
        zm = [sb(f"zm{i}", [128, 128]) for i in range(2)]
        z_hi = [sb(f"z_hi{i}", [128, 128], f32r) for i in range(2)]
        z_lo = [sb(f"z_lo{i}", [128, 128], f32r) for i in range(2)]
        out_sb = [sb(f"out_sb{i}", [128, T]) for i in range(GP)]

        loaded = {n: sem("loaded_" + n) for n in
                  ("wpt", "bwt", "w3t", "a3t", "bmt", "wbase", "wt", "a1t", "scales", "bias", "combo")}
        x_loaded = [sem(f"x_loaded{i}") for i in range(2)]
        w_loaded = [sem(f"w_loaded{i}") for i in range(2)]
        r_loaded = [sem(f"r_loaded{i}") for i in range(2 * GP)]
        out_stored = [sem(f"out_stored{i}") for i in range(GP)]
        idx_loaded = sem("idx_loaded")
        combo_stored = sem("combo_stored")
        table_stored = sem("table_stored")
        own_half_ready = sem("own_half_ready")
        zeroed, const_ready = sem("zeroed"), sem("const_ready")
        combo_ready, onehot_ready, bias_cols_ready = sem("combo_ready"), sem("onehot_ready"), sem("bias_cols_ready")
        n_ready = sem("n_ready")
        q_done, q_ready = sem("q_done"), sem("q_ready")
        qn_done, qn_ready = sem("qn_done"), sem("qn_ready")
        r_done, r_f_ready, r_hi_ready, r_lo_ready = sem("r_done"), sem("r_f_ready"), sem("r_hi_ready"), sem("r_lo_ready")
        n13_done, n13_hi_ready, n13_ready = sem("n13_done"), sem("n13_hi_ready"), sem("n13_ready")
        pg_done, pg_f_ready, pg_hi_ready, pg_ready = sem("pg_done"), sem("pg_f_ready"), sem("pg_hi_ready"), sem("pg_ready")
        bc_done = sem("bc_done")
        dve_self, act_self, pool_self = sem("dve_self"), sem("act_self"), sem("pool_self")
        u_table_ready = sem("u_table_ready")
        w_prepared = sem("w_prepared")
        lb_done, lb_evacuated = sem("lb_done"), sem("lb_evacuated")
        yt_done, y_f_ready, y_hi_ready, y_ready = sem("yt_done"), sem("y_f_ready"), sem("y_hi_ready"), sem("y_ready")
        u_ready = sem("u_ready")
        z_done, zx_ready, zw_ready, zs_ready = sem("z_done"), sem("zx_ready"), sem("zw_ready"), sem("zs_ready")
        zm_ready, z_hi_ready, z_ready = sem("zm_ready"), sem("z_hi_ready"), sem("z_ready")
        out_done, out_copied = sem("out_done"), sem("out_copied")

        chunks = "(k p) n -> p k n"
        x_rows = x.rearrange("b c t -> (b c) t").rearrange("(g j p) t -> g p j t", j=GP, p=128)
        out_rows = out.rearrange("b c t -> (b c) t").rearrange("(q p) t -> q p t", p=128)

        block = ctx.enter_context(nc.Block())

        @block.sync
        def _(sp):
            sp.dma_start(wpt_sb[:], wpt.rearrange(chunks, p=128)).then_inc(loaded["wpt"], 16)
            sp.dma_start(bwt_sb[:], bwt.rearrange(chunks, p=128)).then_inc(loaded["bwt"], 16)
            sp.dma_start(scale1_sb[:, :], scale1.to_broadcast([128, E1])).then_inc(loaded["scales"], 16)
            sp.dma_start(n3_sb[:], w3t.rearrange(chunks, p=128)).then_inc(loaded["w3t"], 16)
            sp.dma_start(a3t_sb[:], a3t.rearrange(chunks, p=128)).then_inc(loaded["a3t"], 16)
            sp.dma_start(q3_sb[:], bmt).then_inc(loaded["bmt"], 16)
            sp.dma_start(wbase_sb[:], wbase.rearrange(chunks, p=128)).then_inc(loaded["wbase"], 16)
            sp.dma_start(wt_sb[:], wt.rearrange(chunks, p=128)).then_inc(loaded["wt"], 16)
            sp.dma_start(a1t_sb[:], a1t.rearrange(chunks, p=128)).then_inc(loaded["a1t"], 16)

            def ask_indices(h_w, h_r):
                if h_w is not None:
                    sp.dma_start(widx_sb[0:1, :, :], idx_w[bass.ds(h_w, 1)]).then_inc(idx_loaded, 16)
                if h_r is not None:
                    sp.dma_start(ridx_sb[0:1, :], combo_dram[bass.ds(h_r, 1)]).then_inc(idx_loaded, 16)

            def fetch_pair_weights(h, parity):
                for n in range(2 * GP):
                    j, half = n // 2, slice(64 * (n % 2), 64 * (n % 2) + 64)
                    s = sp.value_load(widx_sb[0:1, 0, n:n + 1], min_val=0, max_val=NS - 1)
                    sp.dma_start(w0_in[parity][half, j, half],
                                 w0t[bass.ds(s, 1)].rearrange("o d c -> (o d) c")).then_inc(w_loaded[parity], 16)
                    c = sp.value_load(widx_sb[0:1, 1, n:n + 1], min_val=0, max_val=NC - 1)
                    sp.dma_start(w2_in[parity][half, j, half],
                                 w2[bass.ds(c, 1)].rearrange("o d c -> (o d) c")).then_inc(w_loaded[parity], 16)

            def fetch_x(at, parity):
                sp.dma_start(x_sb[parity][:], x_rows[bass.ds(at, 1)].rearrange("o p j t -> (o p) j t")
                             ).then_inc(x_loaded[parity], 16)

            def fetch_r(parity):
                for n in range(2 * GP):
                    j = n // 2
                    combo = sp.value_load(ridx_sb[0:1, n:n + 1], min_val=0, max_val=COMBOS - 1)
                    for hl in range(2):
                        row = 64 * hl + RB * (n % 2)
                        sp.dma_start(r_sb[parity * GP + j][row:row + RB, :].bitcast(f32),
                                     r_table[bass.ds(combo, 1), hl].rearrange("o r n -> (o r) n")
                                     ).then_inc(r_loaded[parity * GP + j], 16)

            ask_indices(0, None)
            sp.wait_ge(idx_loaded, 16)
            sp.wait_ge(zeroed, 4)
            fetch_pair_weights(0, 0)
            fetch_x(0, 0)
            ask_indices(1, None)
            sp.wait_ge(idx_loaded, 32)
            fetch_pair_weights(1, 1)
            sp.wait_ge(combo_stored, 16)
            tables = r_table.rearrange("(ac m) h r n -> ac h m r n", ac=E3 // 2)
            q3_rows = r_table.rearrange("(a e) h r n -> e h a r n", e=E1)
            for hl, (ready, r_part, q3_part) in enumerate(((r_hi_ready, r_hi, q3_hi), (r_lo_ready, r_lo, q3_lo))):
                sp.wait_ge(ready, 5)
                for ac in range(E3 // 2):
                    sp.dma_start(tables[ac, hl, :, 0:RK, :], r_part[:, ac, :].bitcast(f32)).then_inc(table_stored, 16)
                for e in range(E1):
                    sp.dma_start(q3_rows[e, hl, :, RK:RB, :], q3_part[:].bitcast(f32)).then_inc(table_stored, 16)
            ask_indices(None, 0)
            sp.wait_ge(idx_loaded, 48)
            sp.wait_ge(table_stored, 16 * 2 * (E3 // 2 + E1))
            fetch_r(0)
            ask_indices(2, 1)

            def group(h, parity):
                if not before_end(h, 1):
                    return
                need(sp, out_done, GP * h)
                need(sp, yt_done, GP * h)
                need(sp, w_prepared, 3 * h + 3)
                need(sp, idx_loaded, 32 * h + 80)
                fetch_x(h + 1, 1 - parity)
                if before_end(h, 2):
                    fetch_pair_weights(h + 2, parity)
                fetch_r(1 - parity)
                if before_end(h, 2):
                    ask_indices(h + 3, h + 2)

            every_group(nc, EN.SP, group)

        @block.tensor
        def _(pe):
            def accumulate(dst, lhs, rhs, **flags):
                for k in range(KT):
                    last = nc.tensor.matmul(dst, lhs(k), rhs(k), start=(k == 0), stop=(k == KT - 1), **flags)
                return last

            def cols(m):
                return slice(128 * m, 128 * m + 128)

            pe.wait_ge(loaded["wpt"], 16)
            pe.wait_ge(loaded["bwt"], 16)
            for m in range(KT):
                last = accumulate(bank[6][:, 64 * m:64 * m + 64], lambda k: wpt_sb[:, k, cols(m)], lambda k: bwt_sb[:, k, :])
            last.then_inc(q_done, 1)
            pe.wait_ge(n_ready, 2)
            pe.wait_ge(loaded["a3t"], 16)
            pe.wait_ge(q_ready, 1)
            accumulate(bank[7][:, :], lambda k: q_sb[:, k, :, :].rearrange("p a b -> p (a b)"), lambda k: n3_sb[:, k, :])
            accumulate(bank[5][:, 0:64], lambda k: a3t_sb[:, k, :], lambda k: q_sb[:, k, 0, :]).then_inc(qn_done, 1)
            pe.wait_ge(n_ready, 3)
            for m in range(KT):
                accumulate(bank[m][:, :], lambda k: wbase_sb[:, k, cols(m)], lambda k: n3_sb[:, k, :]).then_inc(n13_done, 1)
            for m in range(KT):
                last = accumulate(bank[4][:, cols(m)], lambda k: wbase_sb[:, k, cols(m)], lambda k: a3t_sb[:, k, :])
            last.then_inc(pg_done, 1)
            pe.wait_ge(loaded["wt"], 16)
            pe.wait_ge(loaded["a1t"], 16)
            pe.wait_ge(q_ready, 1)
            for m in range(KT):
                last = accumulate(bank[6][:, 64 * m:64 * m + 64], lambda k: wt_sb[:, k, cols(m)], lambda k: a1t_sb[:, k, :])
            last.then_inc(pg_done, 1)
            pe.wait_ge(onehot_ready, 1)
            pe.wait_ge(qn_ready, 2)
            nc.tensor.matmul(bank[7][:, 0:B], bias_sb[:, :, :].rearrange("s a d -> s (a d)"), onehot[:, :],
                             start=True, stop=True).then_inc(bc_done, 1)
            for ac in range(E3 // 2):
                pe.wait_ge(n13_hi_ready, ac + 1)
                pe.wait_ge(n13_ready, ac + 1)
                nc.tensor.matmul(bank[ac][:, :], qa_sb[:, 2 * ac:2 * ac + 2, :].rearrange("p a b -> p (a b)"),
                                 q3_sb[:, :], start=True, stop=True).then_inc(r_done, 1)

            def channel_products(h, parity):
                need(pe, w_prepared, 3 * (h + 1))
                need(pe, lb_evacuated, 2 * h)
                for j in range(GP):
                    nc.tensor.matmul(l_ps[:, cols(j)], w0_i[parity][:, j, :], w2_i[parity][:, j, :], start=True, stop=True)
                for j in range(GP):
                    last = nc.tensor.matmul(beta_ps[:, cols(j)], bias_b[parity][:, j, :], w2_i[parity][:, j, :],
                                            start=True, stop=True)
                last.then_inc(lb_done, 1)

            def y_product(h, parity, j, uses):
                if j == 0:
                    need(pe, x_loaded[parity], 16 * uses)
                    need(pe, lb_evacuated, 2 * (h + 1))
                need(pe, y_f_ready, GP * h + j - 1)
                for k in range(KT):
                    last = nc.tensor.matmul(yt_ps[j % 2][:, cols(k)], x_sb[parity][:, j, cols(k)], l_sb[parity][:, j, :],
                                            start=True, stop=True)
                last.then_inc(yt_done, 1)

            pe.wait_ge(pg_f_ready, 2)
            pe.wait_ge(bias_cols_ready, 2)
            channel_products(0, 0)
            pe.wait_ge(r_f_ready, 4)
            y_product(0, 0, 0, 1)
            y_product(0, 0, 1, 1)
            pe.wait_ge(n13_hi_ready, KT)
            pe.wait_ge(n13_ready, KT)

            def group(h, parity):
                for j in range(GP):
                    t = GP * h + j
                    even = j % 2
                    need(pe, y_ready, t + 1)
                    need(pe, u_ready, 2 * (t + 1))
                    for k in range(KT):
                        last = nc.tensor.matmul(z_ps[even][:, 0:256],
                                                u_sb[even][:, k, :, :, :].rearrange("p h b r -> p (h b r)"),
                                                y_sb[even][:, k, :, :].rearrange("p h n -> p (h n)"),
                                                start=(k == 0), stop=(k == KT - 1))
                    last.then_inc(z_done, 1)
                    need(pe, out_copied, t - 1)
                    for k in range(KT):
                        for yp, np_ in ((0, 0), (0, 1), (1, 0)):
                            nc.tensor.matmul(out_ps[even][:, :], y_sb[even][:, k, yp, :], n13[:, k, np_, :],
                                             start=(k == 0 and yp == 0 and np_ == 0), stop=False)
                    if j == 0 and before_end(h, 1):
                        channel_products(h + 1, 1 - parity)
                    if j < 2:
                        y_product(h, parity, j + 2, 0)
                    elif before_end(h, 1):
                        y_product(h + 1, 1 - parity, j - 2, group_use(h + 1, 1 - parity))
                    need(pe, z_ready, t + 1)
                    need(pe, r_loaded[parity * GP + j], 64 * group_use(h, parity))
                    nc.tensor.matmul(out_ps[even][:, :], z_hi[even][:, :], r_sb[parity * GP + j][:, :], start=False, stop=False)
                    nc.tensor.matmul(out_ps[even][:, :], z_lo[even][:, :], r_sb[parity * GP + j][:, :],
                                     start=False, stop=True).then_inc(out_done, 1)

            every_group(nc, EN.PE, group)

        @block.scalar
        def _(act):
            act.dma_start(parts_sb[0:1, :, :], combo_parts).then_inc(loaded["combo"], 16)
            act.dma_start(subj_i[:, :], subjects.to_broadcast([NS, B])).then_inc(loaded["bias"], 16)
            for copy in range(2):
                act.dma_start(bias_sb[:, copy, :], bias).then_inc(loaded["bias"], 16)
            for a in range(E3):
                act.dma_start(scale3_sb[RK * a:RK * a + RK, :], scale3[:, a:a + 1].to_broadcast([RK, 1])
                              ).then_inc(loaded["scales"], 16)
            act.wait_ge(combo_ready, 1)
            act.dma_start(combo_dram.rearrange("(o g) n -> o (g n)", o=1), combo_sb[0:1, :]).then_inc(combo_stored, 16)

            act.wait_ge(n_ready, 2)
            nc.scalar.copy(q3_hi[:, :], q3_sb[:, :]).then_inc(r_hi_ready, 1)
            for m in range(KT):
                act.wait_ge(n13_done, m + 1)
                nc.scalar.copy(n13[:, m, 0, :], bank[m][:, :]).then_inc(n13_hi_ready, 1)
            act.wait_ge(pg_f_ready, 2)
            nc.scalar.copy(pg[:, 0, :, :], pg_f[:, :, :]).then_inc(pg_hi_ready, 1)
            for ac in range(E3 // 2):
                act.wait_ge(r_f_ready, ac + 1)
                nc.scalar.copy(r_hi[:, ac, :], r_f[:, ac, :]).then_inc(r_hi_ready, 1)
            act.wait_ge(pg_ready, 1)
            for hl in range(2):
                for k in range(KT):
                    nc.scalar.copy(
                        u_table[:, :, k, hl, 0:RK].rearrange("p (a e) r -> p a e r", e=E1),
                        pg[:, hl, k, 0:E1 * RK].rearrange("p (o e r) -> p o e r", o=1, e=E1).to_broadcast([128, E3, E1, RK])
                    ).then_inc(u_table_ready, 1)

            def y_hi(t, even):
                need(act, y_f_ready, t + 1)
                nc.scalar.copy(y_sb[even][:, :, 0, :], y_f[even][:, :, :]).then_inc(y_hi_ready, 1)

            def copy_out(t, even, slot, stores):
                need(act, out_done, t + 1)
                need(act, out_stored[slot], 16 * stores)
                nc.scalar.copy(out_sb[slot][:, :], out_ps[even][:, :]).then_inc(out_copied, 1)

            def store(t, slot):
                need(act, out_copied, t + 1)
                act.dma_start(out_rows[bass.ds(t, 1)].rearrange("o p t -> (o p) t"), out_sb[slot][:, :]
                              ).then_inc(out_stored[slot], 16)

            y_hi(0, 0)

            def group(h, parity):
                for j in range(GP):
                    t = GP * h + j
                    even = j % 2
                    before = not isinstance(h, int) or t > 0
                    slot, stores = (j - 1) % GP, (h if j else h - 1)
                    if before:
                        copy_out(t - 1, 1 - even, slot, stores)
                    need(act, z_done, t + 1)
                    nc.scalar.copy(zx[even][0:64, :], z_ps[even][64:128, 0:256])
                    nc.scalar.copy(zx[even][64:128, :], z_ps[even][0:64, 0:256]).then_inc(zx_ready, 1)
                    if before_end(h, 0, GROUPS - 1) or j < GP - 1:
                        y_hi(t + 1, 1 - even)
                    need(act, zm_ready, t + 1)
                    nc.scalar.copy(z_hi[even][:, :], zm[even][:, :]).then_inc(z_hi_ready, 1)
                    if before:
                        store(t - 1, slot)

            every_group(nc, EN.Activation, group)
            copy_out(PAIRS - 1, 1, GP - 1, GROUPS - 1)
            store(PAIRS - 1, GP - 1)
            for slot in range(GP):
                act.wait_ge(out_stored[slot], 16 * GROUPS)

        @block.vector
        def _(dve):
            def minus_hi(out_lo, value, hi):
                return nc.vector.tensor_tensor(out_lo, value, hi.bitcast(f32), ALU.subtract)

            for hl in range(2):
                for b in range(2):
                    rows = slice(64 * hl + RB * b, 64 * hl + RB * b + RB)
                    nc.vector.memset(own_half[rows, 64 * b:64 * b + 64], 1.0).then_inc(own_half_ready, 1)
                    nc.vector.memset(own_half[rows, 64 * (1 - b):64 * (1 - b) + 64], 0.0).then_inc(own_half_ready, 1)
            dve.wait_ge(loaded["combo"], 16)
            nc.vector.scalar_tensor_tensor(combo_sb[0:1, :], parts_sb[0:1, 1, :], float(E1), parts_sb[0:1, 0, :],
                                           ALU.mult, ALU.add).then_inc(combo_ready, 1)
            dve.wait_ge(loaded["bias"], 48)
            dve.wait_ge(const_ready, 4)
            nc.vector.tensor_copy(subj_f[:, :], subj_i[:, :]).then_inc(dve_self, 1)
            nc.vector.tensor_copy(row_f[:, :], row_i[:, :]).then_inc(dve_self, 1)
            dve.wait_ge(dve_self, 2)
            nc.vector.tensor_scalar(onehot[:, :], subj_f[:, :], row_f[0:NS, :], None, ALU.is_equal).then_inc(onehot_ready, 1)
            dve.wait_ge(q_done, 1)
            dve.wait_ge(loaded["scales"], 16 * (1 + E3))
            for copy in range(2):
                last = nc.vector.tensor_tensor(
                    q_sb[:, :, copy, :].rearrange("p m (e r) -> p m e r", e=E1),
                    bank[6][:, 0:256].rearrange("p (m e r) -> p m e r", m=KT, e=E1),
                    scale1_sb[:, :].rearrange("p (o e i) -> p o e i", o=1, i=1).to_broadcast([128, KT, E1, RK]), ALU.mult)
            dve.wait_ge(loaded["w3t"], 16)
            for k in range(KT):
                diag = slice(128 * k, 128 * k + 128)
                last2 = nc.vector.tensor_tensor(n3_sb[:, k, diag], n3_sb[:, k, diag], ident[:, :], ALU.add)
            last.then_inc(q_ready, 1)
            last2.then_inc(n_ready, 1)
            dve.wait_ge(loaded["bmt"], 16)
            nc.vector.tensor_scalar(q3_sb[:, :], q3_sb[:, :], scale3_sb[:, 0:1], None, ALU.mult).then_inc(n_ready, 1)
            dve.wait_ge(loaded["wbase"], 16)
            for k in range(KT):
                diag = slice(128 * k, 128 * k + 128)
                last = nc.vector.tensor_tensor(wbase_sb[:, k, diag], wbase_sb[:, k, diag], ident[:, :], ALU.add)
            last.then_inc(n_ready, 1)
            dve.wait_ge(qn_done, 1)
            nc.vector.tensor_copy(qn_sb[:, :], bank[7][:, :]).then_inc(qn_ready, 1)
            nc.vector.tensor_tensor(
                qa_sb[:, :, :], bank[5][:, 0:64].rearrange("p (o r) -> p o r", o=1).to_broadcast([128, E3, E1 * RK]),
                own_adapter[:, :].rearrange("p (a o) -> p a o", o=1).to_broadcast([128, E3, E1 * RK]),
                ALU.mult).then_inc(qn_ready, 1)
            dve.wait_ge(r_hi_ready, 1)
            minus_hi(q3_lo[:, :], q3_sb[:, :], q3_hi[:, :]).then_inc(r_lo_ready, 1)
            for m in range(KT):
                dve.wait_ge(n13_hi_ready, m + 1)
                minus_hi(n13[:, m, 1, :], bank[m][:, :], n13[:, m, 0, :]).then_inc(n13_ready, 1)
            dve.wait_ge(pg_done, 1)
            nc.vector.tensor_copy(pg_f[:, :, E1 * RK:], bank[4][:, :].rearrange("p (m r) -> p m r", m=KT)).then_inc(pg_f_ready, 1)
            dve.wait_ge(pg_done, 2)
            nc.vector.tensor_copy(pg_f[:, :, 0:E1 * RK], bank[6][:, 0:256].rearrange("p (m r) -> p m r", m=KT)).then_inc(pg_f_ready, 1)
            dve.wait_ge(bc_done, 1)
            by_batch = bank[7][:, 0:B].rearrange("p (q b) -> p q b", b=2)
            for b in range(2):
                nc.vector.tensor_copy(bias_cols[64 * b:64 * b + 64, :], by_batch[64 * b:64 * b + 64, :, b]).then_inc(bias_cols_ready, 1)
            for ac in range(E3 // 2):
                dve.wait_ge(r_done, ac + 1)
                dve.wait_ge(qn_ready, 1)
                nc.vector.tensor_tensor(r_f[:, ac, :], bank[ac][:, :], qn_sb[:, :], ALU.add).then_inc(r_f_ready, 1)
            dve.wait_ge(pg_hi_ready, 1)
            dve.wait_ge(pg_f_ready, 2)
            minus_hi(pg[:, 1, :, :], pg_f[:, :, :], pg[:, 0, :, :]).then_inc(pg_ready, 1)
            for ac in range(E3 // 2):
                dve.wait_ge(r_hi_ready, ac + 2)
                minus_hi(r_lo[:, ac, :], r_f[:, ac, :], r_hi[:, ac, :]).then_inc(r_lo_ready, 1)
            dve.wait_ge(pg_ready, 1)
            for hl in range(2):
                for k in range(KT):
                    nc.vector.tensor_copy(
                        u_table[:, :, k, hl, RK:RB].rearrange("p (a e) r -> p a e r", e=E1),
                        pg[:, hl, k, E1 * RK:].rearrange("p (a o r) -> p a o r", o=1, r=RK).to_broadcast([128, E3, E1, RK])
                    ).then_inc(u_table_ready, 1)

            def evacuate_lb(h, parity):
                need(dve, lb_done, h + 1)
                nc.vector.tensor_copy(l_sb[parity][:, :, :], l_ps[:, :].rearrange("p (j n) -> p j n", j=GP)).then_inc(lb_evacuated, 1)
                nc.vector.tensor_copy(beta_sb[parity][:, :, :], beta_ps[:, :].rearrange("p (j n) -> p j n", j=GP)).then_inc(lb_evacuated, 1)

            def y_plus_beta(t, parity, j, h):
                if j == 0:
                    need(dve, lb_evacuated, 2 * (h + 1))
                need(dve, yt_done, t + 1)
                nc.vector.tensor_tensor(
                    y_f[j % 2][:, :, :], yt_ps[j % 2][:, :].rearrange("p (k n) -> p k n", k=KT),
                    beta_sb[parity][:, j:j + 1, :].to_broadcast([128, KT, 128]), ALU.add).then_inc(y_f_ready, 1)

            def y_lo(t, even):
                need(dve, y_hi_ready, t + 1)
                minus_hi(y_sb[even][:, :, 1, :], y_f[even][:, :, :], y_sb[even][:, :, 0, :]).then_inc(y_ready, 1)

            def gather_u(t, even):
                for b in range(2):
                    combo = nc.vector.value_load(combo_sb[0:1, bass.ds(2 * t + b, 1)], min_val=0, max_val=COMBOS - 1)
                    nc.vector.tensor_copy(
                        u_sb[even][:, :, :, b, :],
                        u_table[:, bass.ds(combo, 1), :, :, :].rearrange("p o k h r -> p (o k) h r")).then_inc(u_ready, 1)

            dve.wait_ge(combo_ready, 1)
            dve.wait_ge(u_table_ready, 4 * KT)
            evacuate_lb(0, 0)
            gather_u(0, 0)
            gather_u(1, 1)
            y_plus_beta(0, 0, 0, 0)
            y_lo(0, 0)

            def group(h, parity):
                for j in range(GP):
                    t = GP * h + j
                    even = j % 2
                    more = before_end(h, 0, GROUPS - 1)
                    if j < GP - 1:
                        y_plus_beta(t + 1, parity, j + 1, h)
                    elif more:
                        y_plus_beta(t + 1, 1 - parity, 0, h + 1)
                    need(dve, zx_ready, t + 1)
                    nc.vector.tensor_tensor(zw[even][:, :], z_ps[even][:, 0:256], zx[even][:, :], ALU.add).then_inc(zw_ready, 1)
                    if j < GP - 1 or more:
                        y_lo(t + 1, 1 - even)
                    if j < 2 or more:
                        gather_u(t + 2, even)
                    if j == 1 and more:
                        evacuate_lb(h + 1, 1 - parity)
                    need(dve, z_hi_ready, t + 1)
                    minus_hi(z_lo[even][:, :], zm[even][:, :], z_hi[even][:, :]).then_inc(z_ready, 1)

            every_group(nc, EN.DVE, group)

        @block.gpsimd
        def _(pool):
            nc.gpsimd.memset(ident[:, :], 1.0).then_inc(pool_self, 1)
            nc.gpsimd.memset(own_adapter[:, :], 1.0).then_inc(pool_self, 1)
            pool.wait_ge(pool_self, 2)
            nc.gpsimd.affine_select(out=ident[:, :], in_=ident[:, :], compare_op=ALU.is_equal, fill=0.0, base=0,
                                    pattern=[[-1, 128]], channel_multiplier=1).then_inc(const_ready, 1)
            nc.gpsimd.iota(row_i[:, :], [[0, 1]], channel_multiplier=1).then_inc(const_ready, 1)
            nc.gpsimd.affine_select(out=own_adapter[:, :], in_=own_adapter[:, :], compare_op=ALU.is_ge, fill=0.0, base=0,
                                    pattern=[[-RK, E3]], channel_multiplier=1).then_inc(const_ready, 1)
            pool.wait_ge(const_ready, 3)
            nc.gpsimd.affine_select(out=own_adapter[:, :], in_=own_adapter[:, :], compare_op=ALU.is_ge, fill=0.0, base=RK - 1,
                                    pattern=[[RK, E3]], channel_multiplier=-1).then_inc(const_ready, 1)
            for i in range(2):
                nc.gpsimd.memset(w0_in[i][:, :, :], 0.0).then_inc(zeroed, 1)
                nc.gpsimd.memset(w2_in[i][:, :, :], 0.0).then_inc(zeroed, 1)
            ident_j = ident[:, :].rearrange("p (o n) -> p o n", o=1).to_broadcast([128, GP, 128])

            def add_identity(h, parity, uses, which):
                if which == 0:
                    need(pool, lb_done, h - 1)
                    need(pool, w_loaded[parity], 256 * uses)
                    nc.gpsimd.tensor_tensor(w0_i[parity][:, :, :], w0_in[parity][:, :, :], ident_j, ALU.add).then_inc(w_prepared, 1)
                elif which == 1:
                    nc.gpsimd.tensor_tensor(w2_i[parity][:, :, :], w2_in[parity][:, :, :], ident_j, ALU.add).then_inc(w_prepared, 1)
                else:
                    nc.gpsimd.tensor_copy(bias_b[parity][:, :, :],
                                          bias_cols[:, bass.ds(GP * h, GP)].rearrange("p (j o) -> p j o", o=1)
                                          .to_broadcast([128, GP, 128])).then_inc(w_prepared, 1)

            pool.wait_ge(const_ready, 4)
            pool.wait_ge(bias_cols_ready, 2)
            pool.wait_ge(own_half_ready, 8)
            for h in range(2):
                for which in range(3):
                    add_identity(h, h, 1, which)

            def group(h, parity):
                for j in range(GP):
                    t = GP * h + j
                    even = j % 2
                    need(pool, zw_ready, t + 1)
                    nc.gpsimd.tensor_tensor(zs[even][:, :], zw[even][:, 0:128], zw[even][:, 128:256], ALU.add).then_inc(zs_ready, 1)
                    need(pool, zs_ready, t + 1)
                    nc.gpsimd.tensor_tensor(zm[even][:, :], zs[even][:, :], own_half[:, :], ALU.mult).then_inc(zm_ready, 1)
                    if j and before_end(h, 2):
                        add_identity(h + 2, parity, group_use(h + 2, parity), j - 1)

            every_group(nc, EN.Pool, group)


def kernel(**inputs):
    import concourse.bacc as bacc
    from concourse.bass_utils import run_bass_kernel_spmd

    a = {k: np.asarray(v) for k, v in inputs.items()}
    c = np.ascontiguousarray

    def per_group(v):
        return v.reshape(GROUPS, 2 * GP)

    arrays = {
        "x": a["x"],
        "idx_w": c(np.pad(np.stack([per_group(a["itok_B_0_7"]), per_group(a["itok_B_1_198"])], 1), ((0, 1), (0, 0), (0, 0)))),
        "combo_parts": c(np.stack([a["itok_B_0_3"], a["itok_B_0_6"]])[None]),
        "subjects": c(a["itok_B_0_7"][None]),
        "bias": a["fside_8xS_0"],
        "w0t": c(a["L0_cond_weights"].transpose(0, 2, 1)),
        "w2": a["L2_cond_weights"],
        "wbase": a["L1_cond_W_base"],
        "w3t": c(a["L3_cond_W"].T),
        "wt": a["L1_cond_Wt"],
        "wpt": c(a["L1_cond_Wp"].T),
        "a1t": c(a["L1_cond_A"].reshape(E1 * RK, T).T),
        "bwt": c(a["L1_cond_B_w"].transpose(1, 0, 2).reshape(T, E1 * RK)),
        "a3t": c(a["L3_cond_A"].reshape(E3 * RK, T).T),
        "bmt": c(a["L3_cond_Bm"].transpose(0, 2, 1).reshape(E3 * RK, T)),
        "scale1": c(a["L1_cond_scaling"][None]),
        "scale3": c(a["L3_cond_scalings"][None]),
    }
    nc = bacc.Bacc("TRN2", target_bir_lowering=False, num_devices=1)
    args = [nc.dram_tensor(n, v.shape, mybir.dt.from_np(v.dtype), kind="ExternalInput").ap() for n, v in arrays.items()]
    args.append(nc.dram_tensor("out", (B, C, T), f32, kind="ExternalOutput").ap())
    build(nc, *args)
    r = run_bass_kernel_spmd(nc, [arrays], core_ids=[0])
    return r.results[0]["out"]
```

```python
from contextlib import ExitStack

import concourse.bass as bass
import numpy as np
from concourse import mybir
from concourse.alu_op_type import AluOpType as ALU

B, C, T = 128, 64, 512
NS, NC = 8, 200
E1, E3, RK = 4, 8, 16
COMBOS = E1 * E3
KT = T // 128
RB = 2 * RK
PAIRS = B // 2
GP = 4
GROUPS = PAIRS // GP
PEEL = 2

f32, f32r, i32 = mybir.dt.float32, mybir.dt.float32r, mybir.dt.int32
COPY = mybir.ActivationFunctionType.Copy
EN = mybir.EngineType


def need(engine, semaphore, value):
    if not isinstance(value, int) or value > 0:
        engine.wait_ge(semaphore, value)


def every_group(nc, engine_type, step):
    for h in range(PEEL):
        step(h, h % 2)
    with nc.Fori(PEEL // 2, (GROUPS - PEEL) // 2, engines=(engine_type,)) as two:
        for parity in range(2):
            step(two * 2 + parity, parity)
    for h in range(GROUPS - PEEL, GROUPS):
        step(h, h % 2)


def before_end(h, ahead, end=GROUPS):
    return not isinstance(h, int) or h + ahead < end


def group_use(h, parity):
    return (h + 2 - parity) // 2


def build(nc, x, subjects, conditions, adapters, bias, w0t, w2, wbase, w3t, wt, wpt, a1t, bwt, a3t, bmt,
          scale1, scale3, out):
    r_table = nc.dram_tensor("r_table", [COMBOS, 2, RB, T], f32).ap()
    w2_batch = nc.dram_tensor("w2_batch", [B, C * C], f32).ap()

    ctx = ExitStack()
    with ctx:
        def sb(name, shape, dt=f32):
            return ctx.enter_context(nc.sbuf_tensor(name, shape, dt))

        def sem(name):
            return ctx.enter_context(nc.semaphore(name))

        bank = [ctx.enter_context(nc.psum_tensor(f"bank{i}", [128, 512], f32)) for i in range(8)]
        yt_ps, z_ps, out_ps, l_ps, beta_ps = bank[0:2], bank[2:4], bank[4:6], bank[6], bank[7]

        wbase_sb = sb("wbase_sb", [128, KT, T])
        n3_sb = sb("n3_sb", [128, KT, T])
        wt_sb = sb("wt_sb", [128, KT, T])
        wpt_sb = sb("wpt_sb", [128, KT, T])
        a1t_sb = sb("a1t_sb", [128, KT, E1 * RK])
        bwt_sb = sb("bwt_sb", [128, KT, E1 * RK])
        a3t_sb = sb("a3t_sb", [128, KT, E3 * RK])
        q3_sb = sb("q3_sb", [128, T])
        scale1_sb = sb("scale1_sb", [128, E1])
        scale3_sb = sb("scale3_sb", [128, 1])
        bias_sb = sb("bias_sb", [NS, 2, C])
        subj_i = sb("subj_i", [NS, B], i32)
        subj_f = sb("subj_f", [NS, B])
        cond_sb = sb("cond_sb", [B, 1], i32)
        row_i = sb("row_i", [128, 1], i32)
        row_f = sb("row_f", [128, 1])
        r_row = sb("r_row", [128, 1])
        onehot = sb("onehot", [NS, B])
        adapters_sb = sb("adapters_sb", [128, 2, B], i32)
        combo_sb = sb("combo_sb", [128, B], i32)
        r_rows = sb("r_rows", [128, PAIRS], i32)
        w0_table = sb("w0_table", [128, NS, C])
        ident = sb("ident", [128, 128])
        own_half = sb("own_half", [128, 128])
        own_adapter = sb("own_adapter", [128, E3])
        q_sb = sb("q_sb", [128, KT, 2, E1 * RK])
        qn_sb = sb("qn_sb", [128, T])
        qa_sb = sb("qa_sb", [128, E3, E1 * RK])
        r_f, r_hi, r_lo = wpt_sb[:, :, :], wbase_sb[:, :, :].bitcast(f32r), wt_sb[:, :, :].bitcast(f32r)
        q3_hi = sb("q3_hi", [128, T], f32r)
        q3_lo = sb("q3_lo", [128, T], f32r)
        n13 = sb("n13", [128, KT, 2, T], f32r)
        pg_f = sb("pg_f", [128, KT, (E1 + E3) * RK])
        pg = sb("pg", [128, 2, KT, (E1 + E3) * RK], f32r)
        u_table = sb("u_table", [128, COMBOS, KT, 2, RB], f32r)
        bias_cols = sb("bias_cols", [128, PAIRS])
        x_both = sb("x_both", [128, 2, GP, T])
        x_sb = [x_both[:, i, :, :] for i in range(2)]
        w2_rows = x_both[:, :, :, :].rearrange("p i j t -> p (i j t)")
        w0_i = [sb(f"w0_i{i}", [128, GP, 128]) for i in range(2)]
        w2_i = [sb(f"w2_i{i}", [128, GP, 128]) for i in range(2)]
        bias_b = [sb(f"bias_b{i}", [128, GP, 128]) for i in range(2)]
        l_sb = [sb(f"l_sb{i}", [128, GP, 128]) for i in range(2)]
        beta_sb = [sb(f"beta_sb{i}", [128, GP, 128]) for i in range(2)]
        r_at = [sb(f"r_at{i}", [128, 1], i32) for i in range(GP)]
        r_sb = [sb(f"r_sb{i}", [128, T], f32r) for i in range(2 * GP)]
        y_f = [sb(f"y_f{i}", [128, KT, 128]) for i in range(2)]
        y_sb = [sb(f"y_sb{i}", [128, KT, 2, 128], f32r) for i in range(2)]
        u_sb = [sb(f"u_sb{i}", [128, KT, 2, 2, RB], f32r) for i in range(2)]
        zx = [sb(f"zx{i}", [128, 256]) for i in range(2)]
        zw = [sb(f"zw{i}", [128, 256]) for i in range(2)]
        zs = [sb(f"zs{i}", [128, 128]) for i in range(2)]
        zm = [sb(f"zm{i}", [128, 128]) for i in range(2)]
        z_hi = [sb(f"z_hi{i}", [128, 128], f32r) for i in range(2)]
        z_lo = [sb(f"z_lo{i}", [128, 128], f32r) for i in range(2)]
        out_sb = [sb(f"out_sb{i}", [128, T]) for i in range(GP)]

        loaded = {n: sem("loaded_" + n) for n in
                  ("wpt", "bwt", "w3t", "a3t", "bmt", "wbase", "wt", "a1t", "scales", "bias", "adapters", "cond", "w0")}
        x_loaded = [sem(f"x_loaded{i}") for i in range(2)]
        w2_loaded = [sem(f"w2_loaded{i}") for i in range(2)]
        w2_gathered, w2_plus_i, w2_stored = sem("w2_gathered"), sem("w2_plus_i"), sem("w2_stored")
        r_loaded = [sem(f"r_loaded{i}") for i in range(2 * GP)]
        out_stored = [sem(f"out_stored{i}") for i in range(GP)]
        table_stored = sem("table_stored")
        own_half_ready = sem("own_half_ready")
        zeroed, const_ready = sem("zeroed"), sem("const_ready")
        r_row_ready, r_rows_ready, r_at_ready = sem("r_row_ready"), sem("r_rows_ready"), sem("r_at_ready")
        w0_table_ready = sem("w0_table_ready")
        combo_ready, onehot_ready, bias_cols_ready = sem("combo_ready"), sem("onehot_ready"), sem("bias_cols_ready")
        n_ready = sem("n_ready")
        q_done, q_ready = sem("q_done"), sem("q_ready")
        qn_done, qn_ready = sem("qn_done"), sem("qn_ready")
        r_done, r_f_ready, r_hi_ready, r_lo_ready = sem("r_done"), sem("r_f_ready"), sem("r_hi_ready"), sem("r_lo_ready")
        n13_done, n13_hi_ready, n13_ready = sem("n13_done"), sem("n13_hi_ready"), sem("n13_ready")
        pg_done, pg_f_ready, pg_hi_ready, pg_ready = sem("pg_done"), sem("pg_f_ready"), sem("pg_hi_ready"), sem("pg_ready")
        bc_done = sem("bc_done")
        dve_self, act_self, pool_self = sem("dve_self"), sem("act_self"), sem("pool_self")
        u_table_ready = sem("u_table_ready")
        w0_ready = sem("w0_ready")
        bias_b_ready = sem("bias_b_ready")
        lb_done, lb_evacuated = sem("lb_done"), sem("lb_evacuated")
        yt_done, y_f_ready, y_hi_ready, y_ready = sem("yt_done"), sem("y_f_ready"), sem("y_hi_ready"), sem("y_ready")
        u_ready = sem("u_ready")
        z_done, zx_ready, zw_ready, zs_ready = sem("z_done"), sem("zx_ready"), sem("zw_ready"), sem("zs_ready")
        zm_ready, z_hi_ready, z_ready = sem("zm_ready"), sem("z_hi_ready"), sem("z_ready")
        out_done, out_copied = sem("out_done"), sem("out_copied")

        chunks = "(k p) n -> p k n"
        x_rows = x.rearrange("b c t -> (b c) t").rearrange("(g j p) t -> g p j t", j=GP, p=128)
        out_rows = out.rearrange("b c t -> (b c) t").rearrange("(q p) t -> q p t", p=128)

        block = ctx.enter_context(nc.Block())

        @block.sync
        def _(sp):
            sp.dma_start(wpt_sb[:], wpt.rearrange(chunks, p=128)).then_inc(loaded["wpt"], 16)
            sp.dma_start(bwt_sb[:], bwt.rearrange(chunks, p=128)).then_inc(loaded["bwt"], 16)
            sp.dma_start(scale1_sb[:, :], scale1.to_broadcast([128, E1])).then_inc(loaded["scales"], 16)
            sp.dma_start(n3_sb[:], w3t.rearrange(chunks, p=128)).then_inc(loaded["w3t"], 16)
            sp.dma_start(a3t_sb[:], a3t.rearrange(chunks, p=128)).then_inc(loaded["a3t"], 16)
            sp.dma_start(q3_sb[:], bmt).then_inc(loaded["bmt"], 16)
            sp.dma_start(wbase_sb[:], wbase.rearrange(chunks, p=128)).then_inc(loaded["wbase"], 16)
            sp.dma_start(wt_sb[:], wt.rearrange(chunks, p=128)).then_inc(loaded["wt"], 16)
            sp.dma_start(a1t_sb[:], a1t.rearrange(chunks, p=128)).then_inc(loaded["a1t"], 16)

            def fetch_w2(h, parity):
                for b in range(2):
                    half = slice(64 * b, 64 * b + 64)
                    sp.dma_start(w2_i[parity][half, :, half],
                                 w2_groups[bass.ds(h, 1), b].rearrange("o d j c -> (o d) j c")).then_inc(w2_loaded[parity], 16)

            def fetch_x(h, parity):
                sp.dma_start(x_sb[parity], x_rows[bass.ds(h, 1)].rearrange("o p j t -> (o p) j t")
                             ).then_inc(x_loaded[parity], 16)

            w2_groups = w2_batch.rearrange("(g j b) (d c) -> g b d j c", j=GP, b=2, c=C)
            sp.wait_ge(w2_plus_i, 1)
            sp.dma_start(w2_batch, w2_rows).then_inc(w2_stored, 16)
            sp.wait_ge(w2_stored, 16)
            sp.wait_ge(zeroed, 4)
            fetch_x(0, 0)
            fetch_w2(0, 0)
            fetch_w2(1, 1)
            tables = r_table.rearrange("(ac m) h r n -> ac h m r n", ac=E3 // 2)
            q3_rows = r_table.rearrange("(a e) h r n -> e h a r n", e=E1)
            for hl, (ready, r_part, q3_part) in enumerate(((r_hi_ready, r_hi, q3_hi), (r_lo_ready, r_lo, q3_lo))):
                sp.wait_ge(ready, 5)
                for ac in range(E3 // 2):
                    sp.dma_start(tables[ac, hl, :, 0:RK, :], r_part[:, ac, :].bitcast(f32)).then_inc(table_stored, 16)
                for e in range(E1):
                    sp.dma_start(q3_rows[e, hl, :, RK:RB, :], q3_part[:].bitcast(f32)).then_inc(table_stored, 16)

            def group(h, parity):
                if before_end(h, 1):
                    need(sp, yt_done, GP * h)
                    fetch_x(h + 1, 1 - parity)
                if before_end(h, 2):
                    need(sp, lb_done, h + 1)
                    fetch_w2(h + 2, parity)

            every_group(nc, EN.SP, group)

        @block.tensor
        def _(pe):
            def accumulate(dst, lhs, rhs, **flags):
                for k in range(KT):
                    last = nc.tensor.matmul(dst, lhs(k), rhs(k), start=(k == 0), stop=(k == KT - 1), **flags)
                return last

            def cols(m):
                return slice(128 * m, 128 * m + 128)

            pe.wait_ge(loaded["wpt"], 16)
            pe.wait_ge(loaded["bwt"], 16)
            for m in range(KT):
                last = accumulate(bank[6][:, 64 * m:64 * m + 64], lambda k: wpt_sb[:, k, cols(m)], lambda k: bwt_sb[:, k, :])
            last.then_inc(q_done, 1)
            pe.wait_ge(n_ready, 2)
            pe.wait_ge(loaded["a3t"], 16)
            pe.wait_ge(q_ready, 1)
            accumulate(bank[7][:, :], lambda k: q_sb[:, k, :, :].rearrange("p a b -> p (a b)"), lambda k: n3_sb[:, k, :])
            accumulate(bank[5][:, 0:64], lambda k: a3t_sb[:, k, :], lambda k: q_sb[:, k, 0, :]).then_inc(qn_done, 1)
            pe.wait_ge(n_ready, 3)
            for m in range(KT):
                accumulate(bank[m][:, :], lambda k: wbase_sb[:, k, cols(m)], lambda k: n3_sb[:, k, :]).then_inc(n13_done, 1)
            for m in range(KT):
                last = accumulate(bank[4][:, cols(m)], lambda k: wbase_sb[:, k, cols(m)], lambda k: a3t_sb[:, k, :])
            last.then_inc(pg_done, 1)
            pe.wait_ge(loaded["wt"], 16)
            pe.wait_ge(loaded["a1t"], 16)
            pe.wait_ge(q_ready, 1)
            for m in range(KT):
                last = accumulate(bank[6][:, 64 * m:64 * m + 64], lambda k: wt_sb[:, k, cols(m)], lambda k: a1t_sb[:, k, :])
            last.then_inc(pg_done, 1)
            pe.wait_ge(onehot_ready, 1)
            pe.wait_ge(qn_ready, 2)
            nc.tensor.matmul(bank[7][:, 0:B], bias_sb[:, :, :].rearrange("s a d -> s (a d)"), onehot[:, :],
                             start=True, stop=True).then_inc(bc_done, 1)
            for ac in range(E3 // 2):
                pe.wait_ge(n13_hi_ready, ac + 1)
                pe.wait_ge(n13_ready, ac + 1)
                nc.tensor.matmul(bank[ac][:, :], qa_sb[:, 2 * ac:2 * ac + 2, :].rearrange("p a b -> p (a b)"),
                                 q3_sb[:, :], start=True, stop=True).then_inc(r_done, 1)

            def channel_products(h, parity):
                need(pe, w0_ready, 2 * GP * (h + 1))
                need(pe, w2_loaded[parity], 32 * group_use(h, parity))
                need(pe, bias_b_ready, h + 1)
                need(pe, lb_evacuated, 2 * h)
                for j in range(GP):
                    nc.tensor.matmul(l_ps[:, cols(j)], w0_i[parity][:, j, :], w2_i[parity][:, j, :], start=True, stop=True)
                for j in range(GP):
                    last = nc.tensor.matmul(beta_ps[:, cols(j)], bias_b[parity][:, j, :], w2_i[parity][:, j, :],
                                            start=True, stop=True)
                last.then_inc(lb_done, 1)

            def y_product(h, parity, j, uses):
                if j == 0:
                    need(pe, x_loaded[parity], 16 * uses)
                    need(pe, lb_evacuated, 2 * (h + 1))
                need(pe, y_f_ready, GP * h + j - 1)
                for k in range(KT):
                    last = nc.tensor.matmul(yt_ps[j % 2][:, cols(k)], x_sb[parity][:, j, cols(k)], l_sb[parity][:, j, :],
                                            start=True, stop=True)
                last.then_inc(yt_done, 1)

            pe.wait_ge(pg_f_ready, 2)
            pe.wait_ge(bias_cols_ready, 2)
            channel_products(0, 0)
            pe.wait_ge(r_f_ready, 4)
            y_product(0, 0, 0, 1)
            y_product(0, 0, 1, 1)
            pe.wait_ge(n13_hi_ready, KT)
            pe.wait_ge(n13_ready, KT)

            def group(h, parity):
                for j in range(GP):
                    t = GP * h + j
                    even = j % 2
                    need(pe, y_ready, t + 1)
                    need(pe, u_ready, 2 * (t + 1))
                    for k in range(KT):
                        last = nc.tensor.matmul(z_ps[even][:, 0:256],
                                                u_sb[even][:, k, :, :, :].rearrange("p h b r -> p (h b r)"),
                                                y_sb[even][:, k, :, :].rearrange("p h n -> p (h n)"),
                                                start=(k == 0), stop=(k == KT - 1))
                    last.then_inc(z_done, 1)
                    need(pe, out_copied, t - 1)
                    for k in range(KT):
                        for yp, np_ in ((0, 0), (0, 1), (1, 0)):
                            nc.tensor.matmul(out_ps[even][:, :], y_sb[even][:, k, yp, :], n13[:, k, np_, :],
                                             start=(k == 0 and yp == 0 and np_ == 0), stop=False)
                    if j == 0 and before_end(h, 1):
                        channel_products(h + 1, 1 - parity)
                    if j < 2:
                        y_product(h, parity, j + 2, 0)
                    elif before_end(h, 1):
                        y_product(h + 1, 1 - parity, j - 2, group_use(h + 1, 1 - parity))
                    need(pe, z_ready, t + 1)
                    need(pe, r_loaded[parity * GP + j], 16 * group_use(h, parity))
                    nc.tensor.matmul(out_ps[even][:, :], z_hi[even][:, :], r_sb[parity * GP + j][:, :], start=False, stop=False)
                    nc.tensor.matmul(out_ps[even][:, :], z_lo[even][:, :], r_sb[parity * GP + j][:, :],
                                     start=False, stop=True).then_inc(out_done, 1)

            every_group(nc, EN.PE, group)

        @block.scalar
        def _(act):
            act.dma_start(cond_sb[:, :], conditions).then_inc(loaded["cond"], 16)
            act.dma_start(adapters_sb[:, :, :], adapters.to_broadcast([128, 2, B])).then_inc(loaded["adapters"], 16)
            act.dma_start(subj_i[:, :], subjects.to_broadcast([NS, B])).then_inc(loaded["bias"], 16)
            for copy in range(2):
                act.dma_start(bias_sb[:, copy, :], bias).then_inc(loaded["bias"], 16)
            for a in range(E3):
                act.dma_start(scale3_sb[RK * a:RK * a + RK, :], scale3[:, a:a + 1].to_broadcast([RK, 1])
                              ).then_inc(loaded["scales"], 16)
            for copy in range(2):
                act.dma_start(w0_table[64 * copy:64 * copy + 64, :, :], w0t.rearrange("s d c -> d s c")
                              ).then_inc(loaded["w0"], 16)

            def pair_w0(h, parity, j):
                for b in range(2):
                    half = slice(64 * b, 64 * b + 64)
                    s = nc.scalar.value_load(subj_i[0:1, bass.ds(2 * (GP * h + j) + b, 1)], min_val=0, max_val=NS - 1)
                    nc.scalar.copy(w0_i[parity][half, j, half],
                                   w0_table[half, bass.ds(s, 1), :].rearrange("p o c -> p (o c)")).then_inc(w0_ready, 1)

            act.wait_ge(loaded["bias"], 48)
            act.wait_ge(w0_table_ready, 1)
            act.wait_ge(zeroed, 4)
            for h in range(2):
                for j in range(GP):
                    pair_w0(h, h, j)
            act.wait_ge(n_ready, 2)
            nc.scalar.copy(q3_hi[:, :], q3_sb[:, :]).then_inc(r_hi_ready, 1)
            for m in range(KT):
                act.wait_ge(n13_done, m + 1)
                nc.scalar.copy(n13[:, m, 0, :], bank[m][:, :]).then_inc(n13_hi_ready, 1)
            act.wait_ge(pg_f_ready, 2)
            nc.scalar.copy(pg[:, 0, :, :], pg_f[:, :, :]).then_inc(pg_hi_ready, 1)
            for ac in range(E3 // 2):
                act.wait_ge(r_f_ready, ac + 1)
                nc.scalar.copy(r_hi[:, ac, :], r_f[:, ac, :]).then_inc(r_hi_ready, 1)
            act.wait_ge(pg_ready, 1)
            for hl in range(2):
                for k in range(KT):
                    nc.scalar.copy(
                        u_table[:, :, k, hl, 0:RK].rearrange("p (a e) r -> p a e r", e=E1),
                        pg[:, hl, k, 0:E1 * RK].rearrange("p (o e r) -> p o e r", o=1, e=E1).to_broadcast([128, E3, E1, RK])
                    ).then_inc(u_table_ready, 1)

            def y_hi(t, even):
                need(act, y_f_ready, t + 1)
                nc.scalar.copy(y_sb[even][:, :, 0, :], y_f[even][:, :, :]).then_inc(y_hi_ready, 1)

            def copy_out(t, even, slot, stores):
                need(act, out_done, t + 1)
                need(act, out_stored[slot], 16 * stores)
                nc.scalar.copy(out_sb[slot][:, :], out_ps[even][:, :]).then_inc(out_copied, 1)

            def store(t, slot):
                need(act, out_copied, t + 1)
                act.dma_start(out_rows[bass.ds(t, 1)].rearrange("o p t -> (o p) t"), out_sb[slot][:, :]
                              ).then_inc(out_stored[slot], 16)

            y_hi(0, 0)

            def group(h, parity):
                for j in range(GP):
                    t = GP * h + j
                    even = j % 2
                    before = not isinstance(h, int) or t > 0
                    slot, stores = (j - 1) % GP, (h if j else h - 1)
                    if before:
                        copy_out(t - 1, 1 - even, slot, stores)
                    need(act, z_done, t + 1)
                    nc.scalar.copy(zx[even][0:64, :], z_ps[even][64:128, 0:256])
                    nc.scalar.copy(zx[even][64:128, :], z_ps[even][0:64, 0:256]).then_inc(zx_ready, 1)
                    if before_end(h, 0, GROUPS - 1) or j < GP - 1:
                        y_hi(t + 1, 1 - even)
                    need(act, zm_ready, t + 1)
                    nc.scalar.copy(z_hi[even][:, :], zm[even][:, :]).then_inc(z_hi_ready, 1)
                    if before:
                        store(t - 1, slot)
                    if before_end(h, 2):
                        if j == 0:
                            need(act, lb_done, h + 1)
                        pair_w0(h + 2, parity, j)

            every_group(nc, EN.Activation, group)
            copy_out(PAIRS - 1, 1, GP - 1, GROUPS - 1)
            store(PAIRS - 1, GP - 1)
            for slot in range(GP):
                act.wait_ge(out_stored[slot], 16 * GROUPS)

        @block.vector
        def _(dve):
            def minus_hi(out_lo, value, hi):
                return nc.vector.tensor_tensor(out_lo, value, hi.bitcast(f32), ALU.subtract)

            for i in range(2):
                nc.vector.memset(w0_i[i][:, :, :], 0.0).then_inc(zeroed, 1)
                nc.vector.memset(w2_i[i][:, :, :], 0.0).then_inc(zeroed, 1)
            dve.wait_ge(const_ready, 4)
            for hl in range(2):
                for b in range(2):
                    rows = slice(64 * hl + RB * b, 64 * hl + RB * b + RB)
                    nc.vector.memset(own_half[rows, 64 * b:64 * b + 64], 1.0).then_inc(own_half_ready, 1)
                    nc.vector.memset(own_half[rows, 64 * (1 - b):64 * (1 - b) + 64], 0.0).then_inc(own_half_ready, 1)
            dve.wait_ge(loaded["adapters"], 16)
            nc.vector.scalar_tensor_tensor(combo_sb[:, :], adapters_sb[:, 1, :], float(E1), adapters_sb[:, 0, :],
                                           ALU.mult, ALU.add).then_inc(combo_ready, 1)
            dve.wait_ge(loaded["w0"], 32)
            for copy in range(2):
                half = slice(64 * copy, 64 * copy + 64)
                table = w0_table[half, :, :]
                last = nc.vector.tensor_tensor(table, table, ident[half, half].rearrange("p (o c) -> p o c", o=1)
                                               .to_broadcast([64, NS, C]), ALU.add)
            last.then_inc(w0_table_ready, 1)
            dve.wait_ge(w2_gathered, 16)
            nc.vector.tensor_scalar(w2_rows[:, 0:C * C:C + 1], w2_rows[:, 0:C * C:C + 1], 1.0, None, ALU.add).then_inc(w2_plus_i, 1)
            nc.vector.tensor_copy(row_f[:, :], row_i[:, :]).then_inc(dve_self, 1)
            dve.wait_ge(dve_self, 1)
            dve.wait_ge(combo_ready, 1)
            for hl in range(2):
                for b in range(2):
                    rows = slice(64 * hl + RB * b, 64 * hl + RB * b + RB)
                    nc.vector.tensor_scalar(r_row[rows, :], row_f[rows, :], float(-RB * hl - RB * b), None, ALU.add).then_inc(r_row_ready, 1)
            dve.wait_ge(r_row_ready, 4)
            by_pair = combo_sb[:, :].rearrange("p (q b) -> p q b", b=2)
            for hl in range(2):
                for b in range(2):
                    rows = slice(64 * hl + RB * b, 64 * hl + RB * b + RB)
                    nc.vector.tensor_scalar(r_rows[rows, :], by_pair[rows, :, b], float(2 * RB), r_row[rows, :],
                                            ALU.mult, ALU.add).then_inc(r_rows_ready, 1)
            dve.wait_ge(loaded["bias"], 48)
            nc.vector.tensor_copy(subj_f[:, :], subj_i[:, :]).then_inc(dve_self, 1)
            dve.wait_ge(dve_self, 2)
            nc.vector.tensor_scalar(onehot[:, :], subj_f[:, :], row_f[0:NS, :], None, ALU.is_equal).then_inc(onehot_ready, 1)
            dve.wait_ge(q_done, 1)
            dve.wait_ge(loaded["scales"], 16 * (1 + E3))
            for copy in range(2):
                last = nc.vector.tensor_tensor(
                    q_sb[:, :, copy, :].rearrange("p m (e r) -> p m e r", e=E1),
                    bank[6][:, 0:256].rearrange("p (m e r) -> p m e r", m=KT, e=E1),
                    scale1_sb[:, :].rearrange("p (o e i) -> p o e i", o=1, i=1).to_broadcast([128, KT, E1, RK]), ALU.mult)
            dve.wait_ge(loaded["w3t"], 16)
            for k in range(KT):
                diag = slice(128 * k, 128 * k + 128)
                last2 = nc.vector.tensor_tensor(n3_sb[:, k, diag], n3_sb[:, k, diag], ident[:, :], ALU.add)
            last.then_inc(q_ready, 1)
            last2.then_inc(n_ready, 1)
            dve.wait_ge(loaded["bmt"], 16)
            nc.vector.tensor_scalar(q3_sb[:, :], q3_sb[:, :], scale3_sb[:, 0:1], None, ALU.mult).then_inc(n_ready, 1)
            dve.wait_ge(loaded["wbase"], 16)
            for k in range(KT):
                diag = slice(128 * k, 128 * k + 128)
                last = nc.vector.tensor_tensor(wbase_sb[:, k, diag], wbase_sb[:, k, diag], ident[:, :], ALU.add)
            last.then_inc(n_ready, 1)
            dve.wait_ge(qn_done, 1)
            nc.vector.tensor_copy(qn_sb[:, :], bank[7][:, :]).then_inc(qn_ready, 1)
            nc.vector.tensor_tensor(
                qa_sb[:, :, :], bank[5][:, 0:64].rearrange("p (o r) -> p o r", o=1).to_broadcast([128, E3, E1 * RK]),
                own_adapter[:, :].rearrange("p (a o) -> p a o", o=1).to_broadcast([128, E3, E1 * RK]),
                ALU.mult).then_inc(qn_ready, 1)
            dve.wait_ge(r_hi_ready, 1)
            minus_hi(q3_lo[:, :], q3_sb[:, :], q3_hi[:, :]).then_inc(r_lo_ready, 1)
            for m in range(KT):
                dve.wait_ge(n13_hi_ready, m + 1)
                minus_hi(n13[:, m, 1, :], bank[m][:, :], n13[:, m, 0, :]).then_inc(n13_ready, 1)
            dve.wait_ge(pg_done, 1)
            nc.vector.tensor_copy(pg_f[:, :, E1 * RK:], bank[4][:, :].rearrange("p (m r) -> p m r", m=KT)).then_inc(pg_f_ready, 1)
            dve.wait_ge(pg_done, 2)
            nc.vector.tensor_copy(pg_f[:, :, 0:E1 * RK], bank[6][:, 0:256].rearrange("p (m r) -> p m r", m=KT)).then_inc(pg_f_ready, 1)
            dve.wait_ge(bc_done, 1)
            by_batch = bank[7][:, 0:B].rearrange("p (q b) -> p q b", b=2)
            for b in range(2):
                nc.vector.tensor_copy(bias_cols[64 * b:64 * b + 64, :], by_batch[64 * b:64 * b + 64, :, b]).then_inc(bias_cols_ready, 1)
            for ac in range(E3 // 2):
                dve.wait_ge(r_done, ac + 1)
                dve.wait_ge(qn_ready, 1)
                nc.vector.tensor_tensor(r_f[:, ac, :], bank[ac][:, :], qn_sb[:, :], ALU.add).then_inc(r_f_ready, 1)
            dve.wait_ge(pg_hi_ready, 1)
            dve.wait_ge(pg_f_ready, 2)
            minus_hi(pg[:, 1, :, :], pg_f[:, :, :], pg[:, 0, :, :]).then_inc(pg_ready, 1)
            for ac in range(E3 // 2):
                dve.wait_ge(r_hi_ready, ac + 2)
                minus_hi(r_lo[:, ac, :], r_f[:, ac, :], r_hi[:, ac, :]).then_inc(r_lo_ready, 1)
            dve.wait_ge(pg_ready, 1)
            for hl in range(2):
                for k in range(KT):
                    nc.vector.tensor_copy(
                        u_table[:, :, k, hl, RK:RB].rearrange("p (a e) r -> p a e r", e=E1),
                        pg[:, hl, k, E1 * RK:].rearrange("p (a o r) -> p a o r", o=1, r=RK).to_broadcast([128, E3, E1, RK])
                    ).then_inc(u_table_ready, 1)

            def evacuate_lb(h, parity):
                need(dve, lb_done, h + 1)
                nc.vector.tensor_copy(l_sb[parity][:, :, :], l_ps[:, :].rearrange("p (j n) -> p j n", j=GP)).then_inc(lb_evacuated, 1)
                nc.vector.tensor_copy(beta_sb[parity][:, :, :], beta_ps[:, :].rearrange("p (j n) -> p j n", j=GP)).then_inc(lb_evacuated, 1)

            def y_plus_beta(t, parity, j, h):
                if j == 0:
                    need(dve, lb_evacuated, 2 * (h + 1))
                need(dve, yt_done, t + 1)
                nc.vector.tensor_tensor(
                    y_f[j % 2][:, :, :], yt_ps[j % 2][:, :].rearrange("p (k n) -> p k n", k=KT),
                    beta_sb[parity][:, j:j + 1, :].to_broadcast([128, KT, 128]), ALU.add).then_inc(y_f_ready, 1)

            def y_lo(t, even):
                need(dve, y_hi_ready, t + 1)
                minus_hi(y_sb[even][:, :, 1, :], y_f[even][:, :, :], y_sb[even][:, :, 0, :]).then_inc(y_ready, 1)

            def gather_u(t, even):
                for b in range(2):
                    combo = nc.vector.value_load(combo_sb[0:1, bass.ds(2 * t + b, 1)], min_val=0, max_val=COMBOS - 1)
                    nc.vector.tensor_copy(
                        u_sb[even][:, :, :, b, :],
                        u_table[:, bass.ds(combo, 1), :, :, :].rearrange("p o k h r -> p (o k) h r")).then_inc(u_ready, 1)

            dve.wait_ge(combo_ready, 1)
            dve.wait_ge(u_table_ready, 4 * KT)
            evacuate_lb(0, 0)
            gather_u(0, 0)
            gather_u(1, 1)
            y_plus_beta(0, 0, 0, 0)
            y_lo(0, 0)

            def group(h, parity):
                for j in range(GP):
                    t = GP * h + j
                    even = j % 2
                    more = before_end(h, 0, GROUPS - 1)
                    if j < GP - 1:
                        y_plus_beta(t + 1, parity, j + 1, h)
                    elif more:
                        y_plus_beta(t + 1, 1 - parity, 0, h + 1)
                    need(dve, zx_ready, t + 1)
                    nc.vector.tensor_tensor(zw[even][:, :], z_ps[even][:, 0:256], zx[even][:, :], ALU.add).then_inc(zw_ready, 1)
                    if j < GP - 1 or more:
                        y_lo(t + 1, 1 - even)
                    if j < 2 or more:
                        gather_u(t + 2, even)
                    if j == 1 and more:
                        evacuate_lb(h + 1, 1 - parity)
                    need(dve, z_hi_ready, t + 1)
                    minus_hi(z_lo[even][:, :], zm[even][:, :], z_hi[even][:, :]).then_inc(z_ready, 1)

            every_group(nc, EN.DVE, group)

        @block.gpsimd
        def _(pool):
            pool.wait_ge(loaded["cond"], 16)
            nc.gpsimd.indirect_dma_start(w2_rows, None, w2.rearrange("s d c -> s (d c)"),
                                         bass.IndirectOffsetOnAxis(ap=cond_sb[:, 0:1], axis=0)).then_inc(w2_gathered, 16)
            nc.gpsimd.memset(ident[:, :], 1.0).then_inc(pool_self, 1)
            nc.gpsimd.memset(own_adapter[:, :], 1.0).then_inc(pool_self, 1)
            pool.wait_ge(pool_self, 2)
            nc.gpsimd.affine_select(out=ident[:, :], in_=ident[:, :], compare_op=ALU.is_equal, fill=0.0, base=0,
                                    pattern=[[-1, 128]], channel_multiplier=1).then_inc(const_ready, 1)
            nc.gpsimd.iota(row_i[:, :], [[0, 1]], channel_multiplier=1).then_inc(const_ready, 1)
            nc.gpsimd.affine_select(out=own_adapter[:, :], in_=own_adapter[:, :], compare_op=ALU.is_ge, fill=0.0, base=0,
                                    pattern=[[-RK, E3]], channel_multiplier=1).then_inc(const_ready, 1)
            pool.wait_ge(const_ready, 3)
            nc.gpsimd.affine_select(out=own_adapter[:, :], in_=own_adapter[:, :], compare_op=ALU.is_ge, fill=0.0, base=RK - 1,
                                    pattern=[[RK, E3]], channel_multiplier=-1).then_inc(const_ready, 1)
            def spread_bias(h, parity):
                nc.gpsimd.tensor_copy(bias_b[parity][:, :, :],
                                      bias_cols[:, bass.ds(GP * h, GP)].rearrange("p (j o) -> p j o", o=1)
                                      .to_broadcast([128, GP, 128])).then_inc(bias_b_ready, 1)

            def list_r(t, j):
                nc.gpsimd.tensor_copy(r_at[j][:, :], r_rows[:, bass.ds(t, 1)]).then_inc(r_at_ready, 1)

            def gather_r(parity, j):
                nc.gpsimd.indirect_dma_start(r_sb[parity * GP + j][:, :].bitcast(f32), None, r_table_rows,
                                             bass.IndirectOffsetOnAxis(ap=r_at[j][:, 0:1], axis=0)
                                             ).then_inc(r_loaded[parity * GP + j], 16)

            r_table_rows = r_table.rearrange("m h r n -> (m h r) n")
            pool.wait_ge(const_ready, 4)
            pool.wait_ge(bias_cols_ready, 2)
            pool.wait_ge(own_half_ready, 8)
            for h in range(2):
                spread_bias(h, h)
            pool.wait_ge(r_rows_ready, 4)
            pool.wait_ge(table_stored, 16 * 2 * (E3 // 2 + E1))
            for j in range(GP):
                list_r(j, j)
            pool.wait_ge(r_at_ready, GP)
            for j in range(GP):
                gather_r(0, j)

            def group(h, parity):
                for j in range(GP):
                    t = GP * h + j
                    even = j % 2
                    if before_end(h, 1):
                        need(pool, r_loaded[parity * GP + j], 16 * group_use(h, parity))
                        need(pool, out_done, t - GP + 1)
                        list_r(t + GP, j)
                        need(pool, r_at_ready, t + GP + 1)
                    need(pool, zw_ready, t + 1)
                    nc.gpsimd.tensor_tensor(zs[even][:, :], zw[even][:, 0:128], zw[even][:, 128:256], ALU.add).then_inc(zs_ready, 1)
                    need(pool, zs_ready, t + 1)
                    nc.gpsimd.tensor_tensor(zm[even][:, :], zs[even][:, :], own_half[:, :], ALU.mult).then_inc(zm_ready, 1)
                    if before_end(h, 1):
                        gather_r(1 - parity, j)
                    if j == 1 and before_end(h, 2):
                        need(pool, lb_done, h + 1)
                        spread_bias(h + 2, parity)

            every_group(nc, EN.Pool, group)


def kernel(**inputs):
    import concourse.bacc as bacc
    from concourse.bass_utils import run_bass_kernel_spmd

    a = {k: np.asarray(v) for k, v in inputs.items()}
    c = np.ascontiguousarray

    arrays = {
        "x": a["x"],
        "subjects": c(a["itok_B_0_7"][None]),
        "conditions": c(a["itok_B_1_198"][:, None]),
        "adapters": c(np.stack([a["itok_B_0_3"], a["itok_B_0_6"]])[None]),
        "bias": a["fside_8xS_0"],
        "w0t": c(a["L0_cond_weights"].transpose(0, 2, 1)),
        "w2": a["L2_cond_weights"],
        "wbase": a["L1_cond_W_base"],
        "w3t": c(a["L3_cond_W"].T),
        "wt": a["L1_cond_Wt"],
        "wpt": c(a["L1_cond_Wp"].T),
        "a1t": c(a["L1_cond_A"].reshape(E1 * RK, T).T),
        "bwt": c(a["L1_cond_B_w"].transpose(1, 0, 2).reshape(T, E1 * RK)),
        "a3t": c(a["L3_cond_A"].reshape(E3 * RK, T).T),
        "bmt": c(a["L3_cond_Bm"].transpose(0, 2, 1).reshape(E3 * RK, T)),
        "scale1": c(a["L1_cond_scaling"][None]),
        "scale3": c(a["L3_cond_scalings"][None]),
    }
    nc = bacc.Bacc("TRN2", target_bir_lowering=False, num_devices=1)
    args = [nc.dram_tensor(n, v.shape, mybir.dt.from_np(v.dtype), kind="ExternalInput").ap() for n, v in arrays.items()]
    args.append(nc.dram_tensor("out", (B, C, T), f32, kind="ExternalOutput").ap())
    build(nc, *args)
    r = run_bass_kernel_spmd(nc, [arrays], core_ids=[0])
    return r.results[0]["out"]
```

```python
from contextlib import ExitStack

import concourse.bass as bass
import numpy as np
from concourse import mybir
from concourse.alu_op_type import AluOpType as ALU

B, C, T = 128, 64, 512
NS, NC = 8, 200
E1, E3, RK = 4, 8, 16
COMBOS = E1 * E3
KT = T // 128
RB = 2 * RK
R1_ROWS, Q3_ROWS = COMBOS * RK, E3 * RK
PAIRS = B // 2
GP = 4
GROUPS = PAIRS // GP
TABLE_PARTS = 4
WARM_UP = 10
PEEL = 2

f32, f32r, i32 = mybir.dt.float32, mybir.dt.float32r, mybir.dt.int32
COPY = mybir.ActivationFunctionType.Copy
EN = mybir.EngineType


def need(engine, semaphore, value):
    if not isinstance(value, int) or value > 0:
        engine.wait_ge(semaphore, value)


def every_group(nc, engine_type, step):
    for h in range(PEEL):
        step(h, h % 2)
    with nc.Fori(PEEL // 2, (GROUPS - PEEL) // 2, engines=(engine_type,)) as two:
        for parity in range(2):
            step(two * 2 + parity, parity)
    for h in range(GROUPS - PEEL, GROUPS):
        step(h, h % 2)


def before_end(h, ahead, end=GROUPS):
    return not isinstance(h, int) or h + ahead < end


def group_use(h, parity):
    return (h + 2 - parity) // 2


def build(nc, x, subjects, conditions, adapters, bias, w0t, w2, wbase, w3t, wt, wpt, a1t, bwt, a3t, bmt,
          scale1, scale3, out):
    r_table = nc.dram_tensor("r_table", [2 * (R1_ROWS + Q3_ROWS), T], f32).ap()
    w2_batch = nc.dram_tensor("w2_batch", [B, C * C], f32).ap()

    ctx = ExitStack()
    with ctx:
        def sb(name, shape, dt=f32):
            return ctx.enter_context(nc.sbuf_tensor(name, shape, dt))

        def sem(name):
            return ctx.enter_context(nc.semaphore(name))

        bank = [ctx.enter_context(nc.psum_tensor(f"bank{i}", [128, 512], f32)) for i in range(8)]
        yt_ps, z_ps, out_ps, l_ps, beta_ps = bank[0:2], bank[2:4], bank[4:6], bank[6], bank[7]

        wbase_sb = sb("wbase_sb", [128, KT, T])
        n3_sb = sb("n3_sb", [128, KT, T])
        wt_sb = sb("wt_sb", [128, KT, T])
        wpt_sb = sb("wpt_sb", [128, KT, T])
        a1t_sb = sb("a1t_sb", [128, KT, E1 * RK])
        bwt_sb = sb("bwt_sb", [128, KT, E1 * RK])
        a3t_sb = sb("a3t_sb", [128, KT, E3 * RK])
        q3_sb = sb("q3_sb", [128, T])
        scale1_sb = sb("scale1_sb", [128, E1])
        scale3_sb = sb("scale3_sb", [128, 1])
        bias_sb = sb("bias_sb", [NS, 2, C])
        subj_i = sb("subj_i", [NS, B], i32)
        subj_f = sb("subj_f", [NS, B])
        cond_sb = sb("cond_sb", [B, 1], i32)
        row_i = sb("row_i", [128, 1], i32)
        row_f = sb("row_f", [128, 1])
        second = sb("second", [128, 1])
        r_row = sb("r_row", [128, 3])
        r_of_a = sb("r_of_a", [128, PAIRS])
        onehot = sb("onehot", [NS, B])
        adapters_sb = sb("adapters_sb", [128, 2, B], i32)
        combo_sb = sb("combo_sb", [128, B], i32)
        r_rows = sb("r_rows", [128, PAIRS], i32)
        w0_table = sb("w0_table", [128, NS, C], f32r)
        ident = sb("ident", [128, 128])
        ones = sb("ones", [128, 128])
        ones_r = sb("ones_r", [128, 128], f32r)
        own_half = sb("own_half", [128, 128])
        own_adapter = sb("own_adapter", [128, E3])
        q_sb = sb("q_sb", [128, KT, 2, E1 * RK])
        qn_sb = sb("qn_sb", [128, T])
        qa_sb = sb("qa_sb", [128, E3, E1 * RK])
        q3_hi = sb("q3_hi", [128, T], f32r)
        q3_lo = sb("q3_lo", [128, T], f32r)
        n13 = sb("n13", [128, KT, 2, T], f32r)
        pg_f = sb("pg_f", [128, KT, (E1 + E3) * RK])
        pg = sb("pg", [128, 2, KT, (E1 + E3) * RK], f32r)
        u_table = sb("u_table", [128, COMBOS, KT, 2, RB], f32r)
        r_f = wpt_sb[:, :, :]
        r_hi = u_table[:, 0:8, :, :, :].rearrange("p m k h r -> p (m k h r)").rearrange("p (a n) -> p a n", n=T)
        r_lo = u_table[:, 8:16, :, :, :].rearrange("p m k h r -> p (m k h r)").rearrange("p (a n) -> p a n", n=T)
        bias_cols = sb("bias_cols", [128, B])
        late = sb("late", [128, 2, GP, T])
        w2_rows = late[:, :, :, :].rearrange("p i j t -> p (i j t)")
        x_sb = [sb("x_sb0", [128, GP, T])[:, :, :], late[:, 0, :, :]]
        w0_b = [sb(f"w0_b{i}", [128, GP, 128], f32r) for i in range(2)]
        w2_f = [sb(f"w2_f{i}", [128, GP, 128]) for i in range(2)]
        w2_b = sb("w2_b", [128, GP, 2, 2, C], f32r)
        bw_f = sb("bw_f", [128, GP, 128])
        w0_f = bw_f[:, :, :].rearrange("p j n -> p (j n)").rearrange("p (s c) -> p s c", s=NS)
        bw_b = sb("bw_b", [128, GP, 128], f32r)
        l_sb = [sb(f"l_sb{i}", [128, GP, 128]) for i in range(2)]
        beta_sb = [sb(f"beta_sb{i}", [128, GP, 128]) for i in range(2)]
        r_at = [sb(f"r_at{i}", [128, 1], i32) for i in range(GP)]
        r_sb = [sb(f"r_sb{i}", [128, T], f32r) for i in range(2 * GP)]
        y_f = [sb(f"y_f{i}", [128, KT, 128]) for i in range(2)]
        y_sb = [sb(f"y_sb{i}", [128, KT, 2, 128], f32r) for i in range(2)]
        u_sb = [sb(f"u_sb{i}", [128, KT, 2, 2, RB], f32r) for i in range(2)]
        zx = [sb(f"zx{i}", [128, 256]) for i in range(2)]
        zw = [sb(f"zw{i}", [128, 256]) for i in range(2)]
        zs = [sb(f"zs{i}", [128, 128]) for i in range(2)]
        zm = [sb(f"zm{i}", [128, 128]) for i in range(2)]
        z_hi = [sb(f"z_hi{i}", [128, 128], f32r) for i in range(2)]
        z_lo = [sb(f"z_lo{i}", [128, 128], f32r) for i in range(2)]
        out_sb = [late[:, 1, i, :] for i in range(GP)]

        loaded = {n: sem("loaded_" + n) for n in
                  ("bwt", "w3t", "a3t", "bmt", "wbase", "wt", "a1t", "scales", "bias", "subjects", "adapters", "cond", "w0")}
        wpt_loaded = [sem(f"wpt_loaded{i}") for i in range(2)]
        x_loaded = [sem(f"x_loaded{i}") for i in range(2)]
        w2_loaded = [sem(f"w2_loaded{i}") for i in range(2)]
        w2_first_stored = sem("w2_first_stored")
        w2_gathered, w2_plus_i, w2_stored = sem("w2_gathered"), sem("w2_plus_i"), sem("w2_stored")
        r_loaded = [sem(f"r_loaded{i}") for i in range(2 * GP)]
        out_stored = [sem(f"out_stored{i}") for i in range(GP)]
        table_stored = sem("table_stored")
        own_half_ready = sem("own_half_ready")
        const_ready, zeroed = sem("const_ready"), sem("zeroed")
        r_row_ready, r_rows_ready, r_at_ready = sem("r_row_ready"), sem("r_rows_ready"), sem("r_at_ready")
        w0_f_ready, w0_hi_ready, w0_table_ready = sem("w0_f_ready"), sem("w0_hi_ready"), sem("w0_table_ready")
        w2_hi_ready, w2_b_ready = sem("w2_hi_ready"), sem("w2_b_ready")
        combo_ready, onehot_ready, bias_cols_ready = sem("combo_ready"), sem("onehot_ready"), sem("bias_cols_ready")
        n3_ready, q3_ready, n1_ready = sem("n3_ready"), sem("q3_ready"), sem("n1_ready")
        q_done, q_ready = sem("q_done"), sem("q_ready")
        qa_done, qa_ready = sem("qa_done"), sem("qa_ready")
        qn_done, qn_ready = sem("qn_done"), sem("qn_ready")
        r_done, r_f_ready, r_hi_ready, r_lo_ready = sem("r_done"), sem("r_f_ready"), sem("r_hi_ready"), sem("r_lo_ready")
        n13_done, n13_hi_ready, n13_ready = sem("n13_done"), sem("n13_hi_ready"), sem("n13_ready")
        pg_done, pg_f_ready, pg_hi_ready, pg_ready = sem("pg_done"), sem("pg_f_ready"), sem("pg_hi_ready"), sem("pg_ready")
        bc_done = sem("bc_done")
        dve_self, pool_self = sem("dve_self"), sem("pool_self")
        u_table_ready = sem("u_table_ready")
        w0_ready = sem("w0_ready")
        bw_f_ready, bw_hi_ready, bw_ready = sem("bw_f_ready"), sem("bw_hi_ready"), sem("bw_ready")
        ones_ready, ones_r_ready = sem("ones_ready"), sem("ones_r_ready")
        l_done, l_evacuated = sem("l_done"), sem("l_evacuated")
        beta_done, beta_evacuated = sem("beta_done"), sem("beta_evacuated")
        yt_done, y_f_ready, y_hi_ready, y_ready = sem("yt_done"), sem("y_f_ready"), sem("y_hi_ready"), sem("y_ready")
        u_ready = sem("u_ready")
        z_done, zx_ready, zw_ready, zs_ready = sem("z_done"), sem("zx_ready"), sem("zw_ready"), sem("zs_ready")
        zm_ready, z_hi_ready, z_ready = sem("zm_ready"), sem("z_hi_ready"), sem("z_ready")
        out_done, out_copied = sem("out_done"), sem("out_copied")

        chunks = "(k p) n -> p k n"
        x_rows = x.rearrange("b c t -> (b c) t").rearrange("(g j p) t -> g p j t", j=GP, p=128)
        out_rows = out.rearrange("b c t -> (b c) t").rearrange("(q p) t -> q p t", p=128)

        block = ctx.enter_context(nc.Block())

        @block.sync
        def _(sp):
            sp.dma_start(bwt_sb[:], bwt.rearrange(chunks, p=128)).then_inc(loaded["bwt"], 16)
            for i in range(2):
                chunk = slice(KT // 2 * i, KT // 2 * (i + 1))
                sp.dma_start(wpt_sb[:, chunk, :], wpt.rearrange(chunks, p=128)[:, chunk, :]).then_inc(wpt_loaded[i], 16)
            sp.dma_start(a3t_sb[:], a3t.rearrange(chunks, p=128)).then_inc(loaded["a3t"], 16)
            sp.dma_start(n3_sb[:], w3t.rearrange(chunks, p=128)).then_inc(loaded["w3t"], 16)
            sp.dma_start(q3_sb[:], bmt).then_inc(loaded["bmt"], 16)
            sp.dma_start(wbase_sb[:], wbase.rearrange(chunks, p=128)).then_inc(loaded["wbase"], 16)
            sp.wait_ge(loaded["wbase"], 16)
            sp.dma_start(wt_sb[:], wt.rearrange(chunks, p=128)).then_inc(loaded["wt"], 16)
            sp.dma_start(a1t_sb[:], a1t.rearrange(chunks, p=128)).then_inc(loaded["a1t"], 16)

            def fetch_w2(h, parity):
                for copy in range(2):
                    half = slice(64 * copy, 64 * copy + 64)
                    sp.dma_start(w2_f[parity][half, :, :].rearrange("d j (b c) -> d (j b) c", b=2),
                                 w2_groups[bass.ds(h, 1)].rearrange("o q d c -> (o d) q c")).then_inc(w2_loaded[parity], 16)

            def fetch_x(h, parity):
                sp.dma_start(x_sb[parity], x_rows[bass.ds(h, 1)].rearrange("o p j t -> (o p) j t")
                             ).then_inc(x_loaded[parity], 16)

            r_part1 = r_table[0:2 * R1_ROWS, :].rearrange("(h c p) n -> h c p n", h=2, p=128)
            q3_part2 = r_table[2 * R1_ROWS:, :].rearrange("(h p) n -> h p n", h=2)

            def store_r_table(hl, ready, r_part, q3_part):
                sp.wait_ge(ready, 5)
                sp.dma_start(r_part1[hl].rearrange("c p n -> p c n"), r_part.bitcast(f32)).then_inc(table_stored, 16)
                sp.dma_start(q3_part2[hl], q3_part[:].bitcast(f32)).then_inc(table_stored, 16)

            w2_groups = w2_batch.rearrange("(g q) (d c) -> g q d c", q=2 * GP, c=C)
            first = 2 * 2 * GP
            sp.wait_ge(w2_plus_i, 1)
            sp.dma_start(w2_batch[0:first, :], w2_rows[0:first, :]).then_inc(w2_first_stored, 16)
            store_r_table(0, r_hi_ready, r_hi, q3_hi)
            sp.wait_ge(w2_first_stored, 16)
            fetch_w2(0, 0)
            store_r_table(1, r_lo_ready, r_lo, q3_lo)
            fetch_x(0, 0)
            fetch_w2(1, 1)
            sp.dma_start(w2_batch[first:B, :], w2_rows[first:B, :]).then_inc(w2_stored, 16)
            sp.wait_ge(w2_stored, 16)

            def store(t, slot):
                need(sp, out_copied, t + 1)
                sp.dma_start(out_rows[bass.ds(t, 1)].rearrange("o p t -> (o p) t"), out_sb[slot]
                             ).then_inc(out_stored[slot], 16)

            def group(h, parity):
                for j in range(GP):
                    if j == 0 and before_end(h, 1):
                        need(sp, yt_done, GP * h)
                        fetch_x(h + 1, 1 - parity)
                    if j == 0 and before_end(h, 2):
                        need(sp, bw_f_ready, h + 1)
                        need(sp, w2_b_ready, h + 1)
                        fetch_w2(h + 2, parity)
                    if j or not isinstance(h, int) or h > 0:
                        store(GP * h + j - 1, (j - 1) % GP)

            every_group(nc, EN.SP, group)
            store(PAIRS - 1, GP - 1)
            for slot in range(GP):
                sp.wait_ge(out_stored[slot], 16 * GROUPS)

        @block.tensor
        def _(pe):
            def accumulate(dst, lhs, rhs, **flags):
                for k in range(KT):
                    last = nc.tensor.matmul(dst, lhs(k), rhs(k), start=(k == 0), stop=(k == KT - 1), **flags)
                return last

            def cols(m):
                return slice(128 * m, 128 * m + 128)

            pe.wait_ge(ones_ready, 1)
            for _ in range(WARM_UP):
                nc.tensor.matmul(bank[5][:, 0:128], ones[:, :], ones[:, :], start=True, stop=True)
            pe.wait_ge(loaded["bwt"], 16)
            for half in range(2):
                pe.wait_ge(wpt_loaded[half], 16)
                for m in range(KT):
                    for k in range(KT // 2 * half, KT // 2 * (half + 1)):
                        last = nc.tensor.matmul(
                            bank[m][:, 0:128], wpt_sb[:, k, cols(m)],
                            bwt_sb[:, k, :].rearrange("p (o n) -> p o n", o=1).to_broadcast([128, 2, E1 * RK]),
                            start=(k == 0), stop=(k == KT - 1))
                    if half:
                        last.then_inc(q_done, 1)
            pe.wait_ge(loaded["a3t"], 16)
            pe.wait_ge(q_ready, KT)
            accumulate(bank[5][:, 0:128], lambda k: a3t_sb[:, k, :], lambda k: q_sb[:, k, :, :].rearrange("p a b -> p (a b)")
                       ).then_inc(qa_done, 1)
            for k in range(KT):
                pe.wait_ge(n3_ready, k + 1)
                last = nc.tensor.matmul(bank[7][:, :], q_sb[:, k, :, :].rearrange("p a b -> p (a b)"), n3_sb[:, k, :],
                                        start=(k == 0), stop=(k == KT - 1))
            last.then_inc(qn_done, 1)
            pe.wait_ge(q3_ready, 1)
            pe.wait_ge(qa_ready, 1)
            for ac in range(E3 // 2):
                nc.tensor.matmul(bank[ac][:, :], qa_sb[:, 2 * ac:2 * ac + 2, :].rearrange("p a b -> p (a b)"),
                                 q3_sb[:, :], start=True, stop=True).then_inc(r_done, 1)
            pe.wait_ge(n1_ready, 1)
            for m in range(KT):
                last = accumulate(bank[4][:, cols(m)], lambda k: wbase_sb[:, k, cols(m)], lambda k: a3t_sb[:, k, :])
            last.then_inc(pg_done, 1)

            def n13_product(m, ks=range(KT)):
                if 0 in ks:
                    pe.wait_ge(r_f_ready, m + 1)
                for k in ks:
                    last = nc.tensor.matmul(bank[m][:, :], wbase_sb[:, k, cols(m)], n3_sb[:, k, :],
                                            start=(k == 0), stop=(k == KT - 1))
                if KT - 1 in ks:
                    last.then_inc(n13_done, 1)

            def channel_products(h, parity, part):
                need(pe, w0_ready, 2 * GP * h + GP * (part + 1))
                if part == 0:
                    need(pe, w2_b_ready, h + 1)
                need(pe, l_evacuated, 2 * h + part)
                for j in range(2):
                    last = nc.tensor.matmul(l_ps[:, 256 * j:256 * j + 256], w0_b[parity][:, 2 * part + j, :],
                                            w2_b[:, 2 * part + j, :, :, :].rearrange("p b h c -> p (b h c)"),
                                            start=True, stop=True)
                last.then_inc(l_done, 1)

            def beta_product(h):
                need(pe, bw_ready, h + 1)
                need(pe, beta_evacuated, h)
                nc.tensor.matmul(beta_ps[:, :], ones_r[:, :], bw_b[:, :, :].rearrange("p j n -> p (j n)"),
                                 start=True, stop=True).then_inc(beta_done, 1)

            def y_product(h, parity, j, uses):
                if j == 0:
                    need(pe, x_loaded[parity], 16 * uses)
                    need(pe, l_evacuated, 2 * (h + 1))
                need(pe, y_f_ready, GP * h + j - 1)
                for k in range(KT):
                    last = nc.tensor.matmul(yt_ps[j % 2][:, cols(k)], x_sb[parity][:, j, cols(k)], l_sb[parity][:, j, :],
                                            start=True, stop=True)
                last.then_inc(yt_done, 1)

            n13_product(0)
            pe.wait_ge(loaded["wt"], 16)
            pe.wait_ge(loaded["a1t"], 16)
            for m in range(KT):
                last = accumulate(bank[6][:, 64 * m:64 * m + 64], lambda k: wt_sb[:, k, cols(m)], lambda k: a1t_sb[:, k, :])
            last.then_inc(pg_done, 1)
            pe.wait_ge(onehot_ready, 1)
            pe.wait_ge(loaded["bias"], 32)
            pe.wait_ge(qn_ready, 1)
            nc.tensor.matmul(bank[7][:, 0:B], bias_sb[:, :, :].rearrange("s a d -> s (a d)"), onehot[:, :],
                             start=True, stop=True).then_inc(bc_done, 1)
            n13_product(1)
            pe.wait_ge(pg_f_ready, 2)
            pe.wait_ge(bias_cols_ready, 1)
            pe.wait_ge(ones_r_ready, 1)
            channel_products(0, 0, 0)
            n13_product(2)
            channel_products(0, 0, 1)
            beta_product(0)
            n13_product(3, range(0, KT // 2))
            pe.wait_ge(n13_ready, 2)
            y_product(0, 0, 0, 1)
            n13_product(3, range(KT // 2, KT))
            y_product(0, 0, 1, 1)

            def group(h, parity):
                for j in range(GP):
                    t = GP * h + j
                    even = j % 2
                    if isinstance(h, int) and t == 0:
                        pe.wait_ge(n13_ready, 3)
                    need(pe, y_ready, t + 1)
                    need(pe, u_ready, 2 * (t + 1))
                    for k in range(KT):
                        last = nc.tensor.matmul(z_ps[even][:, 0:256],
                                                u_sb[even][:, k, :, :, :].rearrange("p h b r -> p (h b r)"),
                                                y_sb[even][:, k, :, :].rearrange("p h n -> p (h n)"),
                                                start=(k == 0), stop=(k == KT - 1))
                    last.then_inc(z_done, 1)
                    need(pe, out_copied, t - 1)
                    for k in range(KT):
                        if isinstance(h, int) and t == 0:
                            pe.wait_ge(n13_ready, k + 1)
                        for yp, np_ in ((0, 0), (0, 1), (1, 0)):
                            nc.tensor.matmul(out_ps[even][:, :], y_sb[even][:, k, yp, :], n13[:, k, np_, :],
                                             start=(k == 0 and yp == 0 and np_ == 0), stop=False)
                    if j < 2 and before_end(h, 1):
                        channel_products(h + 1, 1 - parity, j)
                        if j == 0:
                            beta_product(h + 1)
                    if j < 2:
                        y_product(h, parity, j + 2, 0)
                    elif before_end(h, 1):
                        y_product(h + 1, 1 - parity, j - 2, group_use(h + 1, 1 - parity))
                    need(pe, z_ready, t + 1)
                    need(pe, r_loaded[parity * GP + j], 16 * group_use(h, parity))
                    nc.tensor.matmul(out_ps[even][:, :], z_hi[even][:, :], r_sb[parity * GP + j][:, :], start=False, stop=False)
                    nc.tensor.matmul(out_ps[even][:, :], z_lo[even][:, :], r_sb[parity * GP + j][:, :],
                                     start=False, stop=True).then_inc(out_done, 1)

            every_group(nc, EN.PE, group)

        @block.scalar
        def _(act):
            act.dma_start(scale1_sb[:, :], scale1.to_broadcast([128, E1])).then_inc(loaded["scales"], 16)
            act.dma_start(scale3_sb[:, :], scale3).then_inc(loaded["scales"], 16)
            act.dma_start(cond_sb[:, :], conditions).then_inc(loaded["cond"], 16)
            act.dma_start(adapters_sb[:, :, :], adapters.to_broadcast([128, 2, B])).then_inc(loaded["adapters"], 16)
            act.dma_start(subj_i[:, :], subjects.to_broadcast([NS, B])).then_inc(loaded["subjects"], 16)
            for copy in range(2):
                act.dma_start(bias_sb[:, copy, :], bias).then_inc(loaded["bias"], 16)
            for copy in range(2):
                act.dma_start(w0_f[64 * copy:64 * copy + 64, :, :], w0t.rearrange("s d c -> d s c")
                              ).then_inc(loaded["w0"], 16)

            def load_subjects(h, j):
                return [nc.scalar.value_load(subj_i[0:1, bass.ds(2 * (GP * h + j) + b, 1)], min_val=0, max_val=NS - 1)
                        for b in range(2)]

            def pair_w0(subjects_of_pair, parity, j):
                for b in range(2):
                    nc.scalar.copy(w0_b[parity][:, j, 64 * b:64 * b + 64],
                                   w0_table[:, bass.ds(subjects_of_pair[b], 1), :].rearrange("p o c -> p (o c)")
                                   ).then_inc(w0_ready, 1)

            def w2_high(h, parity):
                need(act, w2_loaded[parity], 32 * group_use(h, parity))
                need(act, l_done, 2 * h)
                nc.scalar.copy(w2_b[:, :, :, 0, :], w2_f[parity][:, :, :].rearrange("p j (b c) -> p j b c", b=2)
                               ).then_inc(w2_hi_ready, 1)

            def bw_high(h):
                need(act, bw_f_ready, h + 1)
                need(act, beta_done, h)
                nc.scalar.copy(bw_b[:, :, :], bw_f[:, :, :]).then_inc(bw_hi_ready, 1)

            def n13_high(m):
                act.wait_ge(n13_done, m + 1)
                nc.scalar.copy(n13[:, m, 0, :], bank[m][:, :]).then_inc(n13_hi_ready, 1)

            act.wait_ge(ones_ready, 1)
            nc.scalar.copy(ones_r[:, :], ones[:, :]).then_inc(ones_r_ready, 1)
            act.wait_ge(q3_ready, 1)
            nc.scalar.copy(q3_hi[:, :], q3_sb[:, :]).then_inc(r_hi_ready, 1)
            for ac in range(E3 // 2):
                act.wait_ge(r_f_ready, ac + 1)
                nc.scalar.copy(r_hi[:, ac, :], r_f[:, ac, :]).then_inc(r_hi_ready, 1)
            act.wait_ge(loaded["subjects"], 16)
            act.wait_ge(w0_f_ready, 1)
            nc.scalar.copy(w0_table[:, :, :], w0_f).then_inc(w0_hi_ready, 1)
            act.wait_ge(w0_table_ready, 1)
            for j in range(GP):
                pair_w0(load_subjects(0, j), 0, j)
            n13_high(0)
            for j in range(GP // 2):
                pair_w0(load_subjects(1, j), 1, j)
            act.wait_ge(pg_f_ready, 2)
            nc.scalar.copy(pg[:, 0, :, :], pg_f[:, :, :]).then_inc(pg_hi_ready, 1)
            w2_high(0, 0)
            bw_high(0)
            n13_high(1)
            pair_w0(load_subjects(1, 2), 1, 2)
            act.wait_ge(pg_ready, 1)
            act.wait_ge(table_stored, 16 * TABLE_PARTS)
            for hl in range(2):
                for k in range(KT):
                    nc.scalar.copy(
                        u_table[:, :, k, hl, 0:RK].rearrange("p (a e) r -> p a e r", e=E1),
                        pg[:, hl, k, 0:E1 * RK].rearrange("p (o e r) -> p o e r", o=1, e=E1).to_broadcast([128, E3, E1, RK])
                    ).then_inc(u_table_ready, 1)
            w2_high(1, 1)
            n13_high(2)

            def y_hi(t, even):
                need(act, y_f_ready, t + 1)
                nc.scalar.copy(y_sb[even][:, :, 0, :], y_f[even][:, :, :]).then_inc(y_hi_ready, 1)

            def copy_out(t, even, slot, stores):
                need(act, out_done, t + 1)
                need(act, out_stored[slot], 16 * stores)
                nc.scalar.copy(out_sb[slot], out_ps[even][:, :]).then_inc(out_copied, 1)

            y_hi(0, 0)
            bw_high(1)
            n13_high(3)

            def group(h, parity):
                for j in range(GP):
                    t = GP * h + j
                    even = j % 2
                    before = not isinstance(h, int) or t > 0
                    if before_end(h, 2):
                        subjects_of_pair = load_subjects(h + 2, j)
                    need(act, z_done, t + 1)
                    nc.scalar.copy(zx[even][0:64, :], z_ps[even][64:128, 0:256])
                    nc.scalar.copy(zx[even][64:128, :], z_ps[even][0:64, 0:256]).then_inc(zx_ready, 1)
                    if isinstance(h, int) and t == 1:
                        act.wait_ge(w2_stored, 16)
                    if before:
                        copy_out(t - 1, 1 - even, (j - 1) % GP, (h if j else h - 1))
                    if j == 2 and before_end(h, 2):
                        bw_high(h + 2)
                    if j == 3 and before_end(h, 2):
                        w2_high(h + 2, parity)
                    if before_end(h, 0, GROUPS - 1) or j < GP - 1:
                        y_hi(t + 1, 1 - even)
                    need(act, zm_ready, t + 1)
                    nc.scalar.copy(z_hi[even][:, :], zm[even][:, :]).then_inc(z_hi_ready, 1)
                    if before_end(h, 2):
                        if isinstance(h, int) and t == 0:
                            pair_w0(load_subjects(1, 3), 1, 3)
                        if j == 0:
                            need(act, l_done, 2 * (h + 1))
                        pair_w0(subjects_of_pair, parity, j)

            every_group(nc, EN.Activation, group)
            copy_out(PAIRS - 1, 1, GP - 1, GROUPS - 1)

        @block.vector
        def _(dve):
            def minus_hi(out_lo, value, hi):
                return nc.vector.tensor_tensor(out_lo, value, hi.bitcast(f32), ALU.subtract)

            for i in range(2):
                nc.vector.memset(l_sb[i][:, :, :], 0.0).then_inc(zeroed, 1)
            dve.wait_ge(const_ready, 4)
            nc.vector.tensor_copy(row_f[:, :], row_i[:, :]).then_inc(dve_self, 1)
            nc.vector.reduce_sum(second[:, :], own_adapter[:, 1:E3:2], axis=mybir.AxisListType.X).then_inc(dve_self, 1)
            dve.wait_ge(dve_self, 2)
            for hl in range(2):
                for b in range(2):
                    rows = slice(64 * hl + RB * b, 64 * hl + RB * b + RB)
                    nc.vector.tensor_scalar(r_row[rows, 0:1], second[rows, :],
                                            float(2 * R1_ROWS + hl * (Q3_ROWS - R1_ROWS) - RK),
                                            float(hl * R1_ROWS - 64 * hl - RB * b), ALU.mult, ALU.add).then_inc(r_row_ready, 1)
                    nc.vector.memset(own_half[rows, 64 * b:64 * b + 64], 1.0).then_inc(own_half_ready, 1)
                    nc.vector.memset(own_half[rows, 64 * (1 - b):64 * (1 - b) + 64], 0.0).then_inc(own_half_ready, 1)
            nc.vector.tensor_scalar(r_row[:, 1:2], second[:, :], float(RK - E1 * RK), float(E1 * RK), ALU.mult, ALU.add).then_inc(r_row_ready, 1)
            nc.vector.tensor_scalar(r_row[:, 2:3], second[:, :], float(-RK), float(RK), ALU.mult, ALU.add).then_inc(r_row_ready, 1)
            dve.wait_ge(r_row_ready, 6)
            nc.vector.tensor_tensor(r_row[:, 0:1], r_row[:, 0:1], row_f[:, :], ALU.add).then_inc(r_row_ready, 1)
            dve.wait_ge(r_row_ready, 7)
            dve.wait_ge(loaded["scales"], 32)
            for m in range(KT):
                dve.wait_ge(q_done, m + 1)
                nc.vector.tensor_tensor(
                    q_sb[:, m, :, :].rearrange("p c (e r) -> p c e r", e=E1),
                    bank[m][:, 0:128].rearrange("p (c e r) -> p c e r", e=E1, r=RK),
                    scale1_sb[:, :].rearrange("p (o e i) -> p o e i", o=1, i=1).to_broadcast([128, 2, E1, RK]), ALU.mult
                ).then_inc(q_ready, 1)
            dve.wait_ge(loaded["w3t"], 16)
            for k in range(KT):
                diag = slice(128 * k, 128 * k + 128)
                nc.vector.tensor_tensor(n3_sb[:, k, diag], n3_sb[:, k, diag], ident[:, :], ALU.add).then_inc(n3_ready, 1)
            dve.wait_ge(loaded["bmt"], 16)
            nc.vector.tensor_scalar(q3_sb[:, :], q3_sb[:, :], scale3_sb[:, 0:1], None, ALU.mult).then_inc(q3_ready, 1)
            dve.wait_ge(qa_done, 1)
            nc.vector.tensor_tensor(
                qa_sb[:, :, :], bank[5][:, 0:64].rearrange("p (o r) -> p o r", o=1).to_broadcast([128, E3, E1 * RK]),
                own_adapter[:, :].rearrange("p (a o) -> p a o", o=1).to_broadcast([128, E3, E1 * RK]),
                ALU.mult).then_inc(qa_ready, 1)
            dve.wait_ge(loaded["adapters"], 16)
            nc.vector.scalar_tensor_tensor(combo_sb[:, :], adapters_sb[:, 1, :], float(E1), adapters_sb[:, 0, :],
                                           ALU.mult, ALU.add).then_inc(combo_ready, 1)
            a_by_pair = adapters_sb[:, 1, :].rearrange("p (q b) -> p q b", b=2)
            e_by_pair = adapters_sb[:, 0, :].rearrange("p (q b) -> p q b", b=2)
            for hl in range(2):
                for b in range(2):
                    rows = slice(64 * hl + RB * b, 64 * hl + RB * b + RB)
                    nc.vector.tensor_scalar(r_of_a[rows, :], a_by_pair[rows, :, b], r_row[rows, 1:2], r_row[rows, 0:1],
                                            ALU.mult, ALU.add).then_inc(r_row_ready, 1)
            dve.wait_ge(r_row_ready, 11)
            for hl in range(2):
                for b in range(2):
                    rows = slice(64 * hl + RB * b, 64 * hl + RB * b + RB)
                    nc.vector.scalar_tensor_tensor(r_rows[rows, :], e_by_pair[rows, :, b], r_row[rows, 2:3], r_of_a[rows, :],
                                                   ALU.mult, ALU.add).then_inc(r_rows_ready, 1)
            dve.wait_ge(loaded["subjects"], 16)
            nc.vector.tensor_copy(subj_f[:, :], subj_i[:, :]).then_inc(dve_self, 1)
            dve.wait_ge(dve_self, 3)
            nc.vector.tensor_scalar(onehot[:, :], subj_f[:, :], row_f[0:NS, :], None, ALU.is_equal).then_inc(onehot_ready, 1)
            dve.wait_ge(loaded["wbase"], 16)
            for k in range(KT):
                diag = slice(128 * k, 128 * k + 128)
                last = nc.vector.tensor_tensor(wbase_sb[:, k, diag], wbase_sb[:, k, diag], ident[:, :], ALU.add)
            last.then_inc(n1_ready, 1)
            dve.wait_ge(qn_done, 1)
            nc.vector.tensor_copy(qn_sb[:, :], bank[7][:, :]).then_inc(qn_ready, 1)
            dve.wait_ge(qn_ready, 1)
            for ac in range(E3 // 2):
                dve.wait_ge(r_done, ac + 1)
                nc.vector.tensor_tensor(r_f[:, ac, :], bank[ac][:, :], qn_sb[:, :], ALU.add).then_inc(r_f_ready, 1)
            dve.wait_ge(loaded["w0"], 32)
            for copy in range(2):
                half = slice(64 * copy, 64 * copy + 64)
                table = w0_f[half, :, :]
                last = nc.vector.tensor_tensor(table, table, ident[half, half].rearrange("p (o c) -> p o c", o=1)
                                               .to_broadcast([64, NS, C]), ALU.add)
            last.then_inc(w0_f_ready, 1)
            dve.wait_ge(w0_hi_ready, 1)
            minus_hi(w0_table[64:128, :, :], w0_f[64:128, :, :], w0_table[64:128, :, :]).then_inc(w0_table_ready, 1)
            dve.wait_ge(w2_gathered, 16)
            nc.vector.tensor_scalar(w2_rows[:, 0:C * C:C + 1], w2_rows[:, 0:C * C:C + 1], 1.0, None, ALU.add).then_inc(w2_plus_i, 1)
            dve.wait_ge(r_hi_ready, 1)
            minus_hi(q3_lo[:, :], q3_sb[:, :], q3_hi[:, :]).then_inc(r_lo_ready, 1)
            for ac in range(E3 // 2):
                dve.wait_ge(r_hi_ready, ac + 2)
                minus_hi(r_lo[:, ac, :], r_f[:, ac, :], r_hi[:, ac, :]).then_inc(r_lo_ready, 1)
            def n13_low(m):
                dve.wait_ge(n13_hi_ready, m + 1)
                minus_hi(n13[:, m, 1, :], bank[m][:, :], n13[:, m, 0, :]).then_inc(n13_ready, 1)

            dve.wait_ge(pg_done, 1)
            nc.vector.tensor_copy(pg_f[:, :, E1 * RK:], bank[4][:, :].rearrange("p (m r) -> p m r", m=KT)).then_inc(pg_f_ready, 1)
            n13_low(0)
            dve.wait_ge(pg_done, 2)
            nc.vector.tensor_copy(pg_f[:, :, 0:E1 * RK], bank[6][:, 0:256].rearrange("p (m r) -> p m r", m=KT)).then_inc(pg_f_ready, 1)
            dve.wait_ge(bc_done, 1)
            nc.vector.tensor_copy(bias_cols[:, :], bank[7][:, 0:B]).then_inc(bias_cols_ready, 1)
            dve.wait_ge(pg_hi_ready, 1)
            dve.wait_ge(pg_f_ready, 2)
            minus_hi(pg[:, 1, :, :], pg_f[:, :, :], pg[:, 0, :, :]).then_inc(pg_ready, 1)

            def w2_low(h, parity):
                need(dve, w2_hi_ready, h + 1)
                minus_hi(w2_b[:, :, :, 1, :], w2_f[parity][:, :, :].rearrange("p j (b c) -> p j b c", b=2),
                         w2_b[:, :, :, 0, :]).then_inc(w2_b_ready, 1)

            def bw_low(h):
                need(dve, bw_hi_ready, h + 1)
                minus_hi(bw_b[64:128, :, :], bw_f[64:128, :, :], bw_b[64:128, :, :]).then_inc(bw_ready, 1)

            def evacuate_l(h, parity, part):
                need(dve, l_done, 2 * h + part + 1)
                by_batch = l_ps[:, :].rearrange("p (j b h c) -> p b j c h", j=2, b=2, h=2)
                for b in range(2):
                    half = slice(64 * b, 64 * b + 64)
                    last = nc.vector.reduce_sum(l_sb[parity][half, 2 * part:2 * part + 2, half], by_batch[half, b, :, :, :],
                                                axis=mybir.AxisListType.X)
                last.then_inc(l_evacuated, 1)

            def evacuate_beta(h, parity):
                need(dve, beta_done, h + 1)
                nc.vector.tensor_copy(beta_sb[parity][:, :, :], beta_ps[:, :].rearrange("p (j n) -> p j n", j=GP)).then_inc(beta_evacuated, 1)

            def y_plus_beta(t, parity, j, h):
                if j == 0:
                    need(dve, beta_evacuated, h + 1)
                need(dve, yt_done, t + 1)
                nc.vector.tensor_tensor(
                    y_f[j % 2][:, :, :], yt_ps[j % 2][:, :].rearrange("p (k n) -> p k n", k=KT),
                    beta_sb[parity][:, j:j + 1, :].to_broadcast([128, KT, 128]), ALU.add).then_inc(y_f_ready, 1)

            def y_lo(t, even):
                need(dve, y_hi_ready, t + 1)
                minus_hi(y_sb[even][:, :, 1, :], y_f[even][:, :, :], y_sb[even][:, :, 0, :]).then_inc(y_ready, 1)

            def load_combos(t):
                return [nc.vector.value_load(combo_sb[0:1, bass.ds(2 * t + b, 1)], min_val=0, max_val=COMBOS - 1)
                        for b in range(2)]

            def gather_u(combos, even):
                for b in range(2):
                    nc.vector.tensor_copy(
                        u_sb[even][:, :, :, b, :],
                        u_table[:, bass.ds(combos[b], 1), :, :, :].rearrange("p o k h r -> p (o k) h r")).then_inc(u_ready, 1)

            w2_low(0, 0)
            bw_low(0)
            n13_low(1)
            dve.wait_ge(zeroed, 2)
            evacuate_l(0, 0, 0)
            dve.wait_ge(pg_ready, 1)
            dve.wait_ge(table_stored, 16 * TABLE_PARTS)
            for hl in range(2):
                for k in range(KT):
                    nc.vector.tensor_copy(
                        u_table[:, :, k, hl, RK:RB].rearrange("p (a e) r -> p a e r", e=E1),
                        pg[:, hl, k, E1 * RK:].rearrange("p (a o r) -> p a o r", o=1, r=RK).to_broadcast([128, E3, E1, RK])
                    ).then_inc(u_table_ready, 1)
            evacuate_l(0, 0, 1)
            evacuate_beta(0, 0)
            dve.wait_ge(combo_ready, 1)
            first_combos = [load_combos(t) for t in range(2)]
            y_plus_beta(0, 0, 0, 0)
            dve.wait_ge(u_table_ready, 4 * KT)
            gather_u(first_combos[0], 0)
            n13_low(2)
            y_lo(0, 0)
            gather_u(first_combos[1], 1)
            w2_low(1, 1)
            n13_low(3)
            bw_low(1)

            def group(h, parity):
                for j in range(GP):
                    t = GP * h + j
                    even = j % 2
                    more = before_end(h, 0, GROUPS - 1)
                    if j < 2 or more:
                        combos = load_combos(t + 2)
                    need(dve, zx_ready, t + 1)
                    nc.vector.tensor_tensor(zw[even][:, :], z_ps[even][:, 0:256], zx[even][:, :], ALU.add).then_inc(zw_ready, 1)
                    if j < GP - 1:
                        y_plus_beta(t + 1, parity, j + 1, h)
                    elif more:
                        y_plus_beta(t + 1, 1 - parity, 0, h + 1)
                    if j < 2 or more:
                        gather_u(combos, even)
                    need(dve, z_hi_ready, t + 1)
                    minus_hi(z_lo[even][:, :], zm[even][:, :], z_hi[even][:, :]).then_inc(z_ready, 1)
                    if j < GP - 1 or more:
                        y_lo(t + 1, 1 - even)
                    if j < 2 and more:
                        evacuate_l(h + 1, 1 - parity, j)
                    if j == 1 and more:
                        evacuate_beta(h + 1, 1 - parity)
                    if j == 3 and before_end(h, 2):
                        bw_low(h + 2)
                        w2_low(h + 2, parity)

            every_group(nc, EN.DVE, group)

        @block.gpsimd
        def _(pool):
            nc.gpsimd.memset(ident[:, :], 1.0).then_inc(pool_self, 1)
            nc.gpsimd.memset(ones[:, :], 1.0).then_inc(ones_ready, 1)
            nc.gpsimd.memset(own_adapter[:, :], 1.0).then_inc(pool_self, 1)
            pool.wait_ge(pool_self, 2)
            nc.gpsimd.affine_select(out=ident[:, :], in_=ident[:, :], compare_op=ALU.is_equal, fill=0.0, base=0,
                                    pattern=[[-1, 128]], channel_multiplier=1).then_inc(const_ready, 1)
            nc.gpsimd.iota(row_i[:, :], [[0, 1]], channel_multiplier=1).then_inc(const_ready, 1)
            nc.gpsimd.affine_select(out=own_adapter[:, :], in_=own_adapter[:, :], compare_op=ALU.is_ge, fill=0.0, base=0,
                                    pattern=[[-RK, E3]], channel_multiplier=1).then_inc(const_ready, 1)
            pool.wait_ge(const_ready, 3)
            nc.gpsimd.affine_select(out=own_adapter[:, :], in_=own_adapter[:, :], compare_op=ALU.is_ge, fill=0.0, base=RK - 1,
                                    pattern=[[RK, E3]], channel_multiplier=-1).then_inc(const_ready, 1)
            pool.wait_ge(loaded["cond"], 16)
            pool.wait_ge(loaded["w3t"], 16)
            nc.gpsimd.indirect_dma_start(w2_rows, None, w2.rearrange("s d c -> s (d c)"),
                                         bass.IndirectOffsetOnAxis(ap=cond_sb[:, 0:1], axis=0)).then_inc(w2_gathered, 16)

            def bias_times_w2(h, parity):
                need(pool, w2_loaded[parity], 32 * group_use(h, parity))
                need(pool, bw_ready, h)
                by_batch = "p j (b c) -> p (j b) c"
                nc.gpsimd.tensor_tensor(bw_f[:, :, :].rearrange(by_batch, b=2), w2_f[parity][:, :, :].rearrange(by_batch, b=2),
                                        bias_cols[:, bass.ds(2 * GP * h, 2 * GP)].rearrange("p (q o) -> p q o", o=1)
                                        .to_broadcast([128, 2 * GP, C]), ALU.mult).then_inc(bw_f_ready, 1)

            def list_r(t, j):
                nc.gpsimd.tensor_copy(r_at[j][:, :], r_rows[:, bass.ds(t, 1)]).then_inc(r_at_ready, 1)

            def gather_r(parity, j):
                nc.gpsimd.indirect_dma_start(r_sb[parity * GP + j][:, :].bitcast(f32), None, r_table_rows,
                                             bass.IndirectOffsetOnAxis(ap=r_at[j][:, 0:1], axis=0)
                                             ).then_inc(r_loaded[parity * GP + j], 16)

            r_table_rows = r_table
            pool.wait_ge(r_rows_ready, 4)
            for j in range(GP):
                list_r(j, j)
            pool.wait_ge(bias_cols_ready, 1)
            bias_times_w2(0, 0)
            pool.wait_ge(r_at_ready, GP)
            pool.wait_ge(table_stored, 16 * TABLE_PARTS)
            for j in range(GP):
                gather_r(0, j)
            pool.wait_ge(own_half_ready, 8)
            bias_times_w2(1, 1)

            def group(h, parity):
                for j in range(GP):
                    t = GP * h + j
                    even = j % 2
                    if before_end(h, 1):
                        need(pool, r_loaded[parity * GP + j], 16 * group_use(h, parity))
                        need(pool, out_done, t - GP + 1)
                        list_r(t + GP, j)
                        need(pool, r_at_ready, t + GP + 1)
                    need(pool, zw_ready, t + 1)
                    nc.gpsimd.tensor_tensor(zs[even][:, :], zw[even][:, 0:128], zw[even][:, 128:256], ALU.add).then_inc(zs_ready, 1)
                    need(pool, zs_ready, t + 1)
                    nc.gpsimd.tensor_tensor(zm[even][:, :], zs[even][:, :], own_half[:, :], ALU.mult).then_inc(zm_ready, 1)
                    if before_end(h, 1):
                        gather_r(1 - parity, j)
                    if j == 1 and before_end(h, 2):
                        bias_times_w2(h + 2, parity)

            every_group(nc, EN.Pool, group)


def kernel(**inputs):
    import concourse.bacc as bacc
    from concourse.bass_utils import run_bass_kernel_spmd

    a = {k: np.asarray(v) for k, v in inputs.items()}
    c = np.ascontiguousarray

    arrays = {
        "x": a["x"],
        "subjects": c(a["itok_B_0_7"][None]),
        "conditions": c(a["itok_B_1_198"][:, None]),
        "adapters": c(np.stack([a["itok_B_0_3"], a["itok_B_0_6"]])[None]),
        "bias": a["fside_8xS_0"],
        "w0t": c(a["L0_cond_weights"].transpose(0, 2, 1)),
        "w2": a["L2_cond_weights"],
        "wbase": a["L1_cond_W_base"],
        "w3t": c(a["L3_cond_W"].T),
        "wt": a["L1_cond_Wt"],
        "wpt": c(a["L1_cond_Wp"].T),
        "a1t": c(a["L1_cond_A"].reshape(E1 * RK, T).T),
        "bwt": c(a["L1_cond_B_w"].transpose(1, 0, 2).reshape(T, E1 * RK)),
        "a3t": c(a["L3_cond_A"].reshape(E3 * RK, T).T),
        "bmt": c(a["L3_cond_Bm"].transpose(0, 2, 1).reshape(E3 * RK, T)),
        "scale1": c(a["L1_cond_scaling"][None]),
        "scale3": c(np.repeat(a["L3_cond_scalings"], RK)[:, None]),
    }
    nc = bacc.Bacc("TRN2", target_bir_lowering=False, num_devices=1)
    args = [nc.dram_tensor(n, v.shape, mybir.dt.from_np(v.dtype), kind="ExternalInput").ap() for n, v in arrays.items()]
    args.append(nc.dram_tensor("out", (B, C, T), f32, kind="ExternalOutput").ap())
    build(nc, *args)
    r = run_bass_kernel_spmd(nc, [arrays], core_ids=[0])
    return r.results[0]["out"]
```
